# Optimizing a Trainium2 kernel written in Bass

```python
import numpy as np
import jax
import jax.numpy as jnp

def _softmax(x, axis=-1):
    return jax.nn.softmax(x, axis=axis)

def _gelu(x):
    return jax.nn.gelu(x, approximate=True)

def _silu(x):
    return jax.nn.silu(x)

def _sigmoid(x):
    return jax.nn.sigmoid(x)

def _layernorm(x, axis=-1, eps=1e-05):
    m = jnp.mean(x, axis=axis, keepdims=True)
    v = jnp.var(x, axis=axis, keepdims=True)
    return (x - m) / jnp.sqrt(v + eps)

def _scatter_add(tgt, idx, src, axis=0):
    return tgt.at[idx].add(src)

def _segment_sum(src, seg, n):
    return jax.ops.segment_sum(src, seg, n)
kernel_name = 'mk_cond_resid_d1_seqx_r2_0ffabd'

def setup_inputs(seed: int=0):
    np.random.seed(seed)
    _w = jnp.asarray

    def _rec_inputs():
        import jax
        import jax.numpy as jnp
        _rk = jax.random.key(seed)
        x = -0.0003929 + 0.9999 * jax.random.normal(jax.random.fold_in(_rk, 1), (128, 128, 2048), jnp.float32)
        _lenS = 128 - jax.random.randint(jax.random.fold_in(_rk, 7), (128,), 0, max(1, 128 // 4) + 1, jnp.int32)
        _lenS2 = 128 - jax.random.randint(jax.random.fold_in(_rk, 8), (128,), 0, max(1, 128 // 4) + 1, jnp.int32)
        itok_B_8_3872 = jax.random.randint(jax.random.fold_in(_rk, 11), (128,), 8, 3873, jnp.int32)
        return (x, itok_B_8_3872)
    x, itok_B_8_3872 = _rec_inputs()

    def _L0_cond_setup():
        import math
        import jax, jax.numpy as jnp
        import numpy as np
        H, N, B, L = (128, 64, 16, 2048)
        DT_MIN, DT_MAX = (0.001, 0.1)

        def _get_kernel(log_dt, C, log_A_real, A_imag, length):
            Cc = C[..., 0] + 1j * C[..., 1]
            dt = jnp.exp(log_dt)
            A = -jnp.exp(log_A_real) + 1j * A_imag
            dtA = A * dt[:, None]
            P = dtA[:, :, None] * jnp.arange(length, dtype=jnp.float32)
            Cs = Cc * (jnp.exp(dtA) - 1.0) / A
            K = 2.0 * jnp.einsum('hn,hnl->hl', Cs, jnp.exp(P)).real
            return K
        key = jax.random.key(seed)
        ks = jax.random.split(key, 6)
        u = jax.random.normal(ks[0], (B, H, L), dtype=jnp.float32)
        length = jax.random.randint(ks[1], (B,), 0, L)
        log_dt = jax.random.uniform(ks[2], (H,), dtype=jnp.float32) * (math.log(DT_MAX) - math.log(DT_MIN)) + math.log(DT_MIN)
        C = jax.random.normal(ks[3], (H, N, 2), dtype=jnp.float32)
        log_A_real = jnp.log(0.5 * jnp.ones((H, N), dtype=jnp.float32))
        A_imag = math.pi * jnp.broadcast_to(jnp.arange(N, dtype=jnp.float32), (H, N))
        D = jax.random.normal(ks[4], (H,), dtype=jnp.float32)
        return {'u': u, 'length': length, 'log_dt': log_dt, 'C': C, 'log_A_real': log_A_real, 'A_imag': A_imag, 'D': D}
    _L0_cond_all = _L0_cond_setup()
    _L0_cond_in = {k: v for k, v in _L0_cond_all.items() if k in ('log_dt', 'C', 'log_A_real', 'A_imag', 'D')}
    del _L0_cond_all
    return {'x': x, 'itok_B_8_3872': itok_B_8_3872, 'L0_cond_log_dt': _L0_cond_in['log_dt'], 'L0_cond_C': _L0_cond_in['C'], 'L0_cond_log_A_real': _L0_cond_in['log_A_real'], 'L0_cond_A_imag': _L0_cond_in['A_imag'], 'L0_cond_D': _L0_cond_in['D']}

def reference(x, itok_B_8_3872, L0_cond_log_dt, L0_cond_C, L0_cond_log_A_real, L0_cond_A_imag, L0_cond_D):
    import jax
    import jax.numpy as jnp

    def _L0_cond_ref(u, length, log_dt, C, log_A_real, A_imag, D):
        import math
        import jax, jax.numpy as jnp
        import numpy as np
        H, N, B, L = (128, 64, 16, 2048)
        DT_MIN, DT_MAX = (0.001, 0.1)

        def _get_kernel(log_dt, C, log_A_real, A_imag, length):
            Cc = C[..., 0] + 1j * C[..., 1]
            dt = jnp.exp(log_dt)
            A = -jnp.exp(log_A_real) + 1j * A_imag
            dtA = A * dt[:, None]
            P = dtA[:, :, None] * jnp.arange(length, dtype=jnp.float32)
            Cs = Cc * (jnp.exp(dtA) - 1.0) / A
            K = 2.0 * jnp.einsum('hn,hnl->hl', Cs, jnp.exp(P)).real
            return K
        Bq, Hq, Lq = u.shape
        mask = (jnp.arange(Lq) < length[:, None]).astype(u.dtype)
        u_m = u * mask[:, None, :]
        kernel = _get_kernel(log_dt, C, log_A_real, A_imag, Lq)
        n = 2 * Lq
        k_f = jnp.fft.rfft(kernel, n=n)
        u_f = jnp.fft.rfft(u_m, n=n)
        y = jnp.fft.irfft(u_f * k_f, n=n)[..., :Lq]
        y = y + u_m * D[:, None]
        return y * mask[:, None, :]
    x = x + _L0_cond_ref(x, itok_B_8_3872, L0_cond_log_dt, L0_cond_C, L0_cond_log_A_real, L0_cond_A_imag, L0_cond_D)
    return x

_drawn_inputs = setup_inputs


def setup_inputs(seed=0):
    import zlib

    import numpy as np

    out = dict(_drawn_inputs(seed))
    spreads = {'L0_cond_log_A_real': (-0.6931471824645996, 0.2)}
    factors = {}
    for name, (base, spread) in spreads.items():
        noise = np.random.default_rng([zlib.crc32(name.encode()), seed]).standard_normal(out[name].shape)
        drawn = base * np.exp(spread * noise) if base else spread * noise
        out[name] = jnp.asarray(drawn.astype(out[name].dtype))
    for name, factor in factors.items():
        out[name] = (out[name] * factor).astype(out[name].dtype)
    return out
```

```python
from contextlib import ExitStack

import concourse.bass as bass
from concourse import mybir

F32 = mybir.dt.float32
F32R = mybir.dt.float32r
I32 = mybir.dt.int32
U8 = mybir.dt.uint8
ALU = mybir.AluOpType
ACT = mybir.ActivationFunctionType

P = 128
CH = 256
PI = 3.14159274101257324
PI_BELOW = 3.1415925
HALF_PI = 1.57079637050628662
INV_2PI = 0.159154943091895336
TWO_PI = (6.28125, 0.0019350051879882812, 3.0199159819567e-07)
MAGIC = 12582912.0
LOG2E = 1.44269504088896341
LN2 = (0.693359375, -2.12194440054690583e-4)
EXP_POLY = (1 / 5040, 1 / 720, 1 / 120, 1 / 24, 1 / 6, 1 / 2, 1.0)

UNROLL = 4
AR = 16
AA = 17
NK = AR + AA
PRO_GROUPS = 7
SPLIT_CREDIT = 4
PAD_WRITES = 32
Y_START = 1
Y_CREDIT = 2


def build(nc, x, lengths, log_dt, C, log_A_real, A_imag, D, out):
    B, H, L = x.shape
    N = A_imag.shape[1]
    NCH = L // CH
    NB = L // P
    QUADS = H // UNROLL
    HP = H + UNROLL
    assert B == P and N == 64 and H <= P and H % UNROLL == 0 and QUADS >= 2 and NCH == 8

    ctx = ExitStack()
    with ctx:
        def sb(name, shape, dt=F32):
            return ctx.enter_context(nc.sbuf_tensor(name, shape, dt))

        def sem(name):
            return ctx.enter_context(nc.semaphore(name))

        x_sb = [sb(f"x{r}", [P, L]) for r in range(UNROLL)]
        U = [[sb(f"u{r}{p}", [P, NB, P], F32R) for p in ("hi", "lo")] for r in range(2)]
        S = [[sb(f"s{r}{p}", [P, NCH - 1, P], F32R) for p in ("hi", "lo")] for r in range(2)]
        PK = sb("proj_and_k", [P, UNROLL, 2, 512], F32R)
        T = sb("toeplitz", [P, UNROLL, 2, CH], F32R)
        Q = sb("readout", [P, UNROLL, 2, AA * AR], F32R)
        LAM = sb("decay", [P, UNROLL, 2, P], F32R)
        Wf = sb("powers", [P, UNROLL, CH])
        Qf = sb("readout_f32", [P, UNROLL, AA * AR])
        prod = [sb(f"prod{i}", [P, AA * AR]) for i in range(2)]
        mask = sb("mask", [P, L], U8)
        ident = sb("ident", [P, P])
        sel_re_f = sb("sel_re_f", [P, P])
        sel_re = sb("sel_re", [P, P], F32R)
        fold = sb("fold", [P, N])
        kv = sb("kv", [P, NK])
        half_pi = sb("half_pi", [P, 1])
        minus_re = sb("minus_re", [P, 1])
        zero = sb("zero", [P, 2, P])
        pos = sb("pos", [P, L])
        len_i = sb("len_i", [P, 1], I32)
        len_f = sb("len_f", [P, 1])
        e_in = sb("e_in", [H, 1 + N])
        e_t = [sb(f"e_t{i}", [H, 1 + N]) for i in range(3)]
        e_i = sb("e_i", [H, 1 + N], I32)
        e_out = sb("e_out", [H, 1 + N])
        aim = sb("aim", [H, N])
        c_in = sb("c_in", [H, N, 2])
        par_h = sb("par_h", [H, 4, 2, N])
        pt = [sb(f"pt{i}", [H, N]) for i in range(12)]
        d_in = sb("d_in", [1, H])
        dcol = sb("dcol", [P, HP])
        par = sb("par", [P, 4, HP])
        ang = sb("ang", [P, UNROLL, NK])
        dec = sb("dec", [P, UNROLL, NK])
        turns = sb("turns", [P, UNROLL, NK])
        turns_r = sb("turns_r", [P, UNROLL, NK])
        red = [sb(f"red{i}", [P, UNROLL, NK]) for i in range(4)]
        ared = sb("ared", [P, UNROLL, NK])
        th = sb("th", [P, UNROLL, NK])
        th_u = sb("th_u", [P, UNROLL, NK])
        th_r = sb("th_r", [P, UNROLL, NK])
        mag = sb("mag", [P, UNROLL, NK])
        trig_y = [sb(f"trig_y{i}", [P, UNROLL, AR]) for i in range(2)]
        trig_x = [sb(f"trig_x{i}", [P, UNROLL, AA]) for i in range(2)]
        Y = [sb(f"y_tab{i}", [P, UNROLL, AR]) for i in range(2)]
        X = [sb(f"x_tab{i}", [P, UNROLL, AA]) for i in range(2)]
        XG = [sb(f"xg_tab{i}", [P, UNROLL, AA]) for i in range(2)]
        xprod = [sb(f"xprod{i}", [P, UNROLL, AA]) for i in range(4)]
        lam_f = sb("lam_f", [P, UNROLL, 2])
        lam_s = sb("lam_s", [P, UNROLL, 2, 2], F32R)
        waited = sb("waited", [P, 1])
        ps_split = [ctx.enter_context(nc.psum_tensor(f"ps_split{i}", [P, 512], F32)) for i in range(4)]
        ps_state = [ctx.enter_context(nc.psum_tensor(f"ps_state{i}", [P, 4, P], F32)) for i in range(2)]
        ps_y = [ctx.enter_context(nc.psum_tensor(f"ps_y{i}", [P, 512], F32)) for i in range(2)]
        k_pad = nc.dram_tensor("k_pad", [UNROLL, 2, 2, P + CH], F32, kind="Internal")

        consts_ready = sem("consts_ready")
        params_in = sem("params_in")
        len_in = sem("len_in")
        dve_step = sem("dve_step")
        act_step = sem("act_step")
        act_params = sem("act_params")
        dve_params = sem("dve_params")
        par_transposed = sem("par_transposed")
        par_ready = sem("par_ready")
        mask_consts = sem("mask_consts")
        pool_step = sem("pool_step")
        args_ready = sem("args_ready")
        angles_reduced = sem("angles_reduced")
        trig_ready = sem("trig_ready")
        mag_ready = sem("mag_ready")
        tables_ready = sem("tables_ready")
        lam_ready = sem("lam_ready")
        gen_ready = sem("gen_ready")
        q_hi = sem("q_hi")
        q_split = sem("q_split")
        transposed = sem("transposed")
        hi_done = sem("hi_done")
        splits = sem("splits")
        state_ready = sem("state_ready")
        s_hi = sem("s_hi")
        s_split = sem("s_split")
        y_ready = sem("y_ready")
        y_out = sem("y_out")
        k_written = sem("k_written")
        written = sem("written")
        x_loaded = [sem(f"x_loaded{r}") for r in range(UNROLL)]
        t_loaded = [sem(f"t_loaded{r}") for r in range(UNROLL)]

        def group(h, g):
            missing = max(0, h - (H - 3)) if isinstance(h, int) else 0
            return h * 5 + (PRO_GROUPS + g - missing)

        def bank(u, g, h=None):
            t = PRO_GROUPS + 5 * u + g
            if h is not None and isinstance(h, int):
                t = group(h, g)
            return t % 4

        def each_channel(eng, body):
            with eng.Fori(0, QUADS - 1) as q:
                for u in range(UNROLL):
                    body(q * UNROLL + u, u, False)
            for u in range(UNROLL):
                body(H - UNROLL + u, u, True)

        block = ctx.enter_context(nc.Block())

        @block.sync
        def _(eng):
            eng.dma_start(e_in[:, 0:1], log_dt.rearrange("(h o) -> h o", o=1)).then_inc(params_in, 16)
            eng.dma_start(e_in[:, 1:1 + N], log_A_real[:, :]).then_inc(params_in, 16)
            eng.dma_start(aim[:, :], A_imag[:, :]).then_inc(params_in, 16)
            eng.dma_start(c_in[:, :, :], C[:, :, :]).then_inc(params_in, 16)
            eng.dma_start(d_in[:, :], D.rearrange("(o h) -> o h", o=1)).then_inc(params_in, 16)
            eng.dma_start(len_i[:, :], lengths.rearrange("(b o) -> b o", o=1)).then_inc(len_in, 16)
            for h in range(UNROLL - 1):
                eng.dma_start(x_sb[h][:, :], x[:, h, :]).then_inc(x_loaded[h], 16)
            eng.wait_ge(consts_ready, 1)
            for copy in range(2):
                eng.dma_start(k_pad[:, copy, :, 0:P], zero[0:UNROLL, :, :]).then_inc(written, 16)
            eng.wait_ge(written, PAD_WRITES)

            def toeplitz(h, r, split_value):
                eng.wait_ge(splits, split_value)
                eng.dma_start(k_pad[r, :, :, P:P + CH],
                              PK[0:2, r, :, CH:2 * CH].bitcast(F32)).then_inc(k_written, 16)
                eng.wait_ge(k_written, h * 16 + 16)
                row = k_pad[r, :, :, :]
                for i in range(2):
                    skewed = bass.AP(row.tensor, row.offset + (i * (P + CH) + P),
                                     [[2 * (P + CH) - N, 2], [-1, N], [1, CH]])
                    eng.dma_start(T[:, r, i, :].bitcast(F32), skewed).then_inc(t_loaded[r], 16)

            for h in range(3):
                toeplitz(h, h, SPLIT_CREDIT + h + 1)

            def channel(h, u, last):
                if not last or h + 3 < H:
                    eng.wait_ge(y_ready, h * 4 + Y_START)
                    toeplitz(h + 3, (u + 3) % UNROLL, group(h, 4) + (SPLIT_CREDIT + 1))
                    eng.wait_ge(written, h * 16 + PAD_WRITES)
                    eng.dma_start(x_sb[(u + 3) % UNROLL][:, :], x[:, bass.ds(h + 3, 1), :].rearrange("b o l -> b (o l)")
                                  ).then_inc(x_loaded[(u + 3) % UNROLL], 16)
                eng.wait_ge(y_out, h * 4 + (Y_CREDIT + 4))
                eng.dma_start(out[:, bass.ds(h, 1), :].rearrange("b o l -> b (o l)"), x_sb[u][:, :]).then_inc(written, 16)

            each_channel(eng, channel)
            eng.wait_ge(written, H * 16 + PAD_WRITES)

        @block.gpsimd
        def _(eng):
            eng.memset(zero[:, :, :], 0.0).then_inc(consts_ready, 1)
            eng.memset(ident[:, :], 1.0).then_inc(pool_step, 1)
            eng.memset(sel_re_f[:, :], 1.0).then_inc(pool_step, 1)
            eng.memset(minus_re[:, :], 1.0).then_inc(pool_step, 1)
            eng.wait_ge(pool_step, 3)
            eng.affine_select(ident[:, :], ident[:, :], [[-1, P]], ALU.is_equal, 0.0, base=0,
                              channel_multiplier=1).then_inc(consts_ready, 1)
            eng.affine_select(sel_re_f[:, :], sel_re_f[:, :], [[0, P]], ALU.is_ge, 0.0, base=N - 1,
                              channel_multiplier=-1).then_inc(consts_ready, 1)
            eng.affine_select(minus_re[:, :], minus_re[:, :], [[0, 1]], ALU.is_ge, -1.0, base=-N,
                              channel_multiplier=1).then_inc(consts_ready, 1)
            eng.iota(kv[:, 0:AR], [[1, AR]], base=0, channel_multiplier=0,
                     allow_small_or_imprecise_dtypes=True).then_inc(consts_ready, 1)
            eng.iota(kv[:, AR:NK], [[AR, AA]], base=0, channel_multiplier=0,
                     allow_small_or_imprecise_dtypes=True).then_inc(consts_ready, 1)
            eng.memset(half_pi[:, :], HALF_PI).then_inc(consts_ready, 1)
            eng.iota(pos[:, :], [[1, L]], base=0, channel_multiplier=0,
                     allow_small_or_imprecise_dtypes=True).then_inc(mask_consts, 1)
            eng.wait_ge(consts_ready, 7)
            eng.tensor_tensor(fold[:, :], ident[:, 0:N], ident[:, N:P], ALU.add).then_inc(pool_step, 1)
            eng.wait_ge(pool_step, 4)

            def times(out_, a, b):
                return eng.tensor_tensor(out_, a, b, ALU.mult)

            def arguments(quad):
                cols = bass.ds(quad * UNROLL, UNROLL)
                k = kv[:, :].unsqueeze(1).broadcast_to([P, UNROLL, NK])
                times(ang[:, :, :], par[:, 1, cols].unsqueeze(2).broadcast_to([P, UNROLL, NK]), k).then_inc(args_ready, 1)
                times(dec[:, :, :], par[:, 0, cols].unsqueeze(2).broadcast_to([P, UNROLL, NK]), k).then_inc(args_ready, 1)

            def tables(quad, done):
                cols = bass.ds(quad * UNROLL, UNROLL)
                eng.wait_ge(trig_ready, done * 7 + 7)
                eng.wait_ge(mag_ready, done + 1)
                if isinstance(done, int) and done == 0:
                    pass
                else:
                    eng.wait_ge(lam_ready, done * 2)
                for i in range(2):
                    times(Y[i][:, :, :], trig_y[i][:, :, :], mag[:, :, 0:AR]).then_inc(pool_step, 1)
                    times(X[i][:, :, :], trig_x[i][:, :, :], mag[:, :, AR:NK]).then_inc(pool_step, 1)
                eng.wait_ge(pool_step, done * 8 + 8)
                g1 = par[:, 2, cols].unsqueeze(2).broadcast_to([P, UNROLL, AA])
                g2 = par[:, 3, cols].unsqueeze(2).broadcast_to([P, UNROLL, AA])
                times(xprod[0][:, :, :], X[0][:, :, :], g1).then_inc(pool_step, 1)
                times(xprod[1][:, :, :], X[1][:, :, :], g2).then_inc(pool_step, 1)
                times(xprod[2][:, :, :], X[1][:, :, :], g1).then_inc(pool_step, 1)
                times(xprod[3][:, :, :], X[0][:, :, :], g2).then_inc(pool_step, 1)
                eng.wait_ge(pool_step, done * 8 + 12)
                eng.tensor_tensor(XG[0][:, :, :], xprod[0][:, :, :], xprod[1][:, :, :], ALU.add).then_inc(tables_ready, 1)
                eng.tensor_tensor(XG[1][:, :, :], xprod[2][:, :, :], xprod[3][:, :, :], ALU.subtract).then_inc(tables_ready, 1)
                eng.wait_ge(tables_ready, done * 2 + 2)

            gen_step = sem("gen_step")

            def matrices(h, r, quad_no):
                def outer(dst, hi, n, step):
                    hi_b = [hi[i][:, r, 0:n].unsqueeze(2).broadcast_to([P, n, AR]) for i in range(2)]
                    lo_b = [Y[i][:, r, :].unsqueeze(1).broadcast_to([P, n, AR]) for i in range(2)]
                    for i in range(2):
                        times(prod[i][:, 0:n * AR].rearrange("p (a r) -> p a r", r=AR), hi_b[i], lo_b[i]).then_inc(gen_step, 1)
                    eng.wait_ge(gen_step, h * 6 + (step + 2))
                    return eng.tensor_tensor(dst, prod[0][:, 0:n * AR], prod[1][:, 0:n * AR], ALU.add).then_inc(gen_step, 1)
                forward = Wf[:, r, :]
                backward = bass.AP(forward.tensor, forward.offset + (CH - 1), [list(forward.ap[0]), [-1, CH]])
                outer(backward, X, AA - 1, 0)
                eng.wait_ge(gen_step, h * 6 + 3)
                outer(Qf[:, r, :], XG, AA, 3)
                eng.wait_ge(gen_step, h * 6 + 6)
                eng.tensor_tensor(Qf[:, r, 0:1], Qf[:, r, 0:1], dcol[:, bass.ds(h, 1)], ALU.add).then_inc(gen_ready, 1)
                eng.wait_ge(lam_ready, quad_no * 2 + 2)

                v = lam_s[:, r, :, :].bitcast(F32).unsqueeze(3).broadcast_to([P, 2, 2, N])
                m = fold[:, :].unsqueeze(1).broadcast_to([P, 2, N])
                for i in range(2):
                    ins = times(LAM[:, r, i, :].rearrange("p (a m) -> p a m", a=2), m, v[:, i, :, :])
                    ins.then_inc(gen_ready, 1)

            eng.wait_ge(par_ready, 3)
            arguments(0)
            tables(0, 0)
            for h in range(UNROLL):
                matrices(h, h, 0)
            arguments(1)
            tables(1, 1)

            def channel(h, u, quad):
                eng.wait_ge(splits, h * 5 + (SPLIT_CREDIT + 1))
                eng.wait_ge(state_ready, h * 7 + 7)
                matrices(h + 4, u, quad + 1)
                if u == 2:
                    arguments(quad + 2)
                if u == 3:
                    tables(quad + 2, quad + 2)

            with eng.Fori(0, QUADS - 1) as q:
                for u in range(UNROLL):
                    channel(q * UNROLL + u, u, q)

        @block.scalar
        def _(eng):
            def angle_tables(done):
                eng.wait_ge(args_ready, done * 2 + 2)
                eng.activation(th[:, :, :], dec[:, :, :], ACT.Tanh, scale=0.5).then_inc(trig_ready, 1)
                eng.wait_ge(angles_reduced, done + 1)
                eng.activation(ared[:, :, :], red[3][:, :, :], ACT.Abs).then_inc(act_step, 1)
                eng.wait_ge(act_step, done + 1)
                def cos(dst, rows, ks):
                    eng.activation(dst[rows, :, :], ared[rows, :, ks], ACT.Sin, bias=half_pi[rows, :], scale=-1.0).then_inc(trig_ready, 1)
                def sin(dst, rows, ks, scale):
                    eng.activation(dst[rows, :, :], red[3][rows, :, ks], ACT.Sin, scale=scale).then_inc(trig_ready, 1)
                re, im, low, high = slice(0, N), slice(N, P), slice(0, AR), slice(AR, NK)
                cos(trig_y[0], re, low)
                sin(trig_y[0], im, low, 1.0)
                sin(trig_y[1], re, low, 1.0)
                cos(trig_y[1], im, low)
                cos(trig_x[0], slice(0, P), high)
                sin(trig_x[1], slice(0, P), high, minus_re[:, 0:1])

            eng.wait_ge(consts_ready, 7)
            eng.activation(sel_re[:, :], sel_re_f[:, :], ACT.Copy).then_inc(act_params, 1)
            eng.wait_ge(dve_params, 1)
            eng.activation(pt[0][:, :], par_h[:, 0, 0, :], ACT.Tanh, scale=0.5).then_inc(act_params, 1)
            eng.wait_ge(dve_params, 2)
            eng.activation(pt[4][:, :], pt[3][:, :], ACT.Abs).then_inc(act_params, 1)
            eng.activation(pt[5][:, :], pt[3][:, :], ACT.Sin).then_inc(act_params, 1)
            eng.activation(pt[6][:, :], pt[3][:, :], ACT.Sin, scale=0.5).then_inc(act_params, 1)
            eng.wait_ge(act_params, 3)
            eng.activation(pt[7][:, :], pt[4][:, :], ACT.Sin, bias=half_pi[0:H, :], scale=-1.0).then_inc(act_params, 1)
            angle_tables(0)

            def split_hi(t, b, dst):
                eng.wait_ge(transposed, t + 1)
                eng.activation(dst, ps_split[b][:, :], ACT.Copy).then_inc(hi_done, 1)

            def q_hi_of(h, r):
                eng.wait_ge(gen_ready, h * 3 + 1)
                eng.activation(Q[:, r, 0, :], Qf[:, r, :], ACT.Copy).then_inc(q_hi, 1)

            def state_hi(count, c, ring):
                eng.wait_ge(state_ready, count)
                eng.activation(S[ring][0][:, c, :], ps_state[c // 4][:, c % 4, :], ACT.Copy).then_inc(s_hi, 1)

            def u_hi(g, ring):
                return U[ring][0][:, 4 * g:4 * g + 4, :].rearrange("p j b -> p (j b)")

            for h in range(3):
                q_hi_of(h, h)
                split_hi(h, h % 4, PK[:, h, 0, :])
            for g in range(4):
                split_hi(3 + g, (3 + g) % 4, u_hi(g, 0))
            state_hi(1, 0, 0)
            angle_tables(1)

            def channel(h, u, last, quad):
                eng.wait_ge(y_ready, h * 4 + Y_START)
                nxt, gen = not last or h + 1 < H, not last or h + 3 < H
                for c in range(NCH):
                    if c < NCH - 2:
                        state_hi(h * 7 + (c + 2), c + 1, u % 2)
                    if c == 0 and gen:
                        q_hi_of(h + 3, (u + 3) % UNROLL)
                    if c < 4 and nxt:
                        split_hi(group(h, c), bank(u, c, h), u_hi(c, (u + 1) % 2))
                    if c == 4 and gen:
                        split_hi(group(h, 4), bank(u, 4, h), PK[:, (u + 3) % UNROLL, 0, :])
                    if c == 5 and nxt:
                        state_hi(h * 7 + 8, 0, (u + 1) % 2)
                    if c == 6 and u == 3 and not last:
                        angle_tables(quad + 2)

            with eng.Fori(0, QUADS - 1) as q:
                for u in range(UNROLL):
                    channel(q * UNROLL + u, u, False, q)
            for u in range(UNROLL):
                channel(H - UNROLL + u, u, True, None)

        @block.vector
        def _(eng):
            count = [0]

            def step(ins):
                count[0] += 1
                ins.then_inc(dve_step, 1)
                eng.wait_ge(dve_step, count[0])

            def reduce_angle(ang_, t0, t1, r, wait):
                wait(eng.tensor_scalar(t0, ang_, INV_2PI, MAGIC, ALU.mult, ALU.add))
                wait(eng.tensor_scalar(t1, t0, MAGIC, None, ALU.subtract))
                src = ang_
                for i in range(3):
                    wait(eng.scalar_tensor_tensor(r[i], t1, -TWO_PI[i], src, ALU.mult, ALU.add))
                    src = r[i]
                return eng.tensor_scalar(r[3], r[2], PI_BELOW, -PI_BELOW, ALU.min, ALU.max)

            eng.memset(dcol[:, :], 0.0).then_inc(dve_step, 1)
            eng.memset(par[:, :, :], 0.0).then_inc(dve_step, 1)
            count[0] = 2
            eng.wait_ge(params_in, 80)
            e, f, n_ = (t[:, :] for t in e_t)
            step(eng.tensor_scalar(e_in[:, :], e_in[:, :], 88.0, -87.0, ALU.min, ALU.max))
            step(eng.tensor_scalar(f, e_in[:, :], LOG2E, MAGIC, ALU.mult, ALU.add))
            step(eng.tensor_scalar(n_, f, MAGIC, None, ALU.subtract))
            step(eng.scalar_tensor_tensor(e, n_, -LN2[0], e_in[:, :], ALU.mult, ALU.add))
            step(eng.scalar_tensor_tensor(e_in[:, :], n_, -LN2[1], e, ALU.mult, ALU.add))
            step(eng.tensor_scalar(f, e_in[:, :], EXP_POLY[0], None, ALU.mult))
            for a in EXP_POLY[1:]:
                step(eng.scalar_tensor_tensor(f, f, a, e_in[:, :], ALU.add, ALU.mult))
            step(eng.tensor_scalar(f, f, 1.0, None, ALU.add))
            step(eng.tensor_scalar(n_, n_, 127.0, 8388608.0, ALU.add, ALU.mult))
            step(eng.tensor_copy(e_i[:, :], n_))
            step(eng.tensor_tensor(e_out[:, :], f, e_i[:, :].bitcast(F32), ALU.mult))
            dt, aexp = e_out[:, 0:1], e_out[:, 1:1 + N]
            p = [t[:, :] for t in pt]
            step(eng.tensor_scalar(p[8], aexp, -1.0, None, ALU.mult))
            step(eng.tensor_scalar(par_h[:, 1, 0, :], aim[:, :], dt, None, ALU.mult))
            eng.tensor_scalar(par_h[:, 0, 0, :], p[8], dt, None, ALU.mult).then_inc(dve_params, 1)
            reduce_angle(par_h[:, 1, 0, :], p[1], p[2], [p[9], p[10], p[11], p[3]], step).then_inc(dve_params, 1)
            eng.wait_ge(act_params, 6)
            step(eng.tensor_scalar(p[1], p[0], -1.0, 1.0, ALU.mult, ALU.add))
            step(eng.reciprocal(p[2], p[1]))
            step(eng.scalar_tensor_tensor(p[1], p[0], 2.0, p[2], ALU.mult, ALU.mult))
            step(eng.scalar_tensor_tensor(p[2], p[1], 1.0, p[5], ALU.add, ALU.mult))
            step(eng.tensor_tensor(p[1], p[1], p[7], ALU.mult))
            step(eng.scalar_tensor_tensor(p[3], p[6], -2.0, p[6], ALU.mult, ALU.mult))
            step(eng.tensor_tensor(p[1], p[1], p[3], ALU.add))
            step(eng.tensor_tensor(p[5], p[8], p[8], ALU.mult))
            step(eng.tensor_tensor(p[6], aim[:, :], aim[:, :], ALU.mult))
            step(eng.tensor_tensor(p[5], p[5], p[6], ALU.add))
            step(eng.reciprocal(p[7], p[5]))
            step(eng.tensor_tensor(p[3], p[1], p[8], ALU.mult))
            step(eng.tensor_tensor(p[4], p[2], aim[:, :], ALU.mult))
            step(eng.tensor_tensor(p[3], p[3], p[4], ALU.add))
            step(eng.tensor_tensor(p[3], p[3], p[7], ALU.mult))
            step(eng.tensor_tensor(p[5], p[2], p[8], ALU.mult))
            step(eng.tensor_tensor(p[6], p[1], aim[:, :], ALU.mult))
            step(eng.tensor_tensor(p[5], p[5], p[6], ALU.subtract))
            step(eng.tensor_tensor(p[4], p[5], p[7], ALU.mult))
            cre, cim = c_in[:, :, 0:1].rearrange("h n o -> h (n o)"), c_in[:, :, 1:2].rearrange("h n o -> h (n o)")
            step(eng.tensor_tensor(p[5], cre, p[3], ALU.mult))
            step(eng.tensor_tensor(p[6], cim, p[4], ALU.mult))
            step(eng.tensor_tensor(p[5], p[5], p[6], ALU.subtract))
            step(eng.tensor_tensor(p[9], cre, p[4], ALU.mult))
            step(eng.tensor_tensor(p[10], cim, p[3], ALU.mult))
            step(eng.tensor_tensor(p[9], p[9], p[10], ALU.add))
            eng.tensor_scalar(par_h[:, 2, 0, :], p[5], 2.0, None, ALU.mult).then_inc(dve_params, 1)
            eng.tensor_scalar(par_h[:, 2, 1, :], p[5], -2.0, None, ALU.mult).then_inc(dve_params, 1)
            for half in range(2):
                eng.tensor_scalar(par_h[:, 3, half, :], p[9], 2.0, None, ALU.mult).then_inc(dve_params, 1)
            for i in range(2):
                eng.tensor_copy(par_h[:, i, 1, :], par_h[:, i, 0, :]).then_inc(dve_params, 1)
            eng.tensor_scalar(dcol[0:1, 0:H], d_in[:, :], 1.0, None, ALU.add).then_inc(par_ready, 1)
            eng.wait_ge(par_transposed, 4)
            eng.tensor_copy(par[:, :, 0:H], ps_split[0][:, 0:4 * H].rearrange("p (i h) -> p i h", i=4)).then_inc(par_ready, 2)
            eng.wait_ge(par_ready, 3)
            eng.memset(th_u[:, 0, 0:1], 0.0).then_inc(splits, SPLIT_CREDIT)
            eng.memset(th_u[:, 0, 1:2], 0.0).then_inc(y_out, Y_CREDIT)

            tab_step = sem("tab_step")

            def reduce_tables(done):
                n = [0]

                def wait(ins):
                    n[0] += 1
                    ins.then_inc(tab_step, 1)
                    eng.wait_ge(tab_step, done * 7 + n[0])
                eng.wait_ge(args_ready, done * 2 + 2)
                reduce_angle(ang[:, :, :], turns[:, :, :], turns_r[:, :, :], [r[:, :, :] for r in red], wait
                             ).then_inc(angles_reduced, 1)

            def magnitudes(done):
                eng.wait_ge(trig_ready, done * 7 + 1)
                eng.tensor_scalar(th_u[:, :, :], th[:, :, :], -1.0, 1.0, ALU.mult, ALU.add).then_inc(tab_step, 1)
                eng.wait_ge(tab_step, done * 7 + 6)
                eng.reciprocal(th_r[:, :, :], th_u[:, :, :]).then_inc(tab_step, 1)
                eng.wait_ge(tab_step, done * 7 + 7)
                eng.scalar_tensor_tensor(mag[:, :, :], th[:, :, :], 1.0, th_r[:, :, :], ALU.add, ALU.mult).then_inc(mag_ready, 1)

            lam_step = sem("lam_step")

            def decay_scalars(done):
                eng.wait_ge(tables_ready, done * 2 + 2)
                if not (isinstance(done, int) and done == 0):
                    eng.wait_ge(gen_ready, done * 12)
                re, im, k256 = slice(0, N), slice(N, P), slice(AA - 1, AA)
                eng.tensor_copy(lam_f[re, :, 0:1], X[0][re, :, k256]).then_inc(lam_step, 1)
                eng.tensor_scalar(lam_f[im, :, 0:1], X[1][im, :, k256], -1.0, None, ALU.mult).then_inc(lam_step, 1)
                eng.tensor_scalar(lam_f[re, :, 1:2], X[1][re, :, k256], -1.0, None, ALU.mult).then_inc(lam_step, 1)
                eng.tensor_copy(lam_f[im, :, 1:2], X[0][im, :, k256]).then_inc(lam_step, 1)
                eng.wait_ge(lam_step, done * 4 + 4)
                eng.tensor_copy(lam_s[:, :, 0, :], lam_f[:, :, :]).then_inc(lam_ready, 1)
                eng.wait_ge(lam_ready, done * 2 + 1)
                eng.tensor_tensor(lam_s[:, :, 1, :], lam_f[:, :, :], lam_s[:, :, 0, :].bitcast(F32), ALU.subtract).then_inc(lam_ready, 1)

            def split_lo(t, b, dst, hi):
                eng.wait_ge(hi_done, t + 1)
                eng.tensor_tensor(dst, ps_split[b][:, :], hi.bitcast(F32), ALU.subtract).then_inc(splits, 1)

            def q_lo_of(h, r):
                eng.wait_ge(q_hi, h + 1)
                eng.tensor_tensor(Q[:, r, 1, :], Qf[:, r, :], Q[:, r, 0, :].bitcast(F32), ALU.subtract).then_inc(q_split, 1)

            def state_lo(count_, c, ring):
                eng.wait_ge(s_hi, count_)
                eng.tensor_tensor(S[ring][1][:, c, :], ps_state[c // 4][:, c % 4, :], S[ring][0][:, c, :].bitcast(F32),
                                  ALU.subtract).then_inc(s_split, 1)

            def u_part(g, ring, half):
                return U[ring][half][:, 4 * g:4 * g + 4, :].rearrange("p j b -> p (j b)")

            def u_lo(t, b, g, ring):
                split_lo(t, b, u_part(g, ring, 1), u_part(g, ring, 0))

            reduce_tables(0)
            magnitudes(0)
            decay_scalars(0)
            eng.wait_ge(len_in, 16)
            eng.wait_ge(mask_consts, 1)
            eng.tensor_copy(len_f[:, :], len_i[:, :]).then_inc(mask_consts, 1)
            eng.wait_ge(mask_consts, 2)
            eng.tensor_scalar(mask[:, :], pos[:, :], len_f[:, 0:1], None, ALU.is_lt).then_inc(mask_consts, 1)
            eng.wait_ge(mask_consts, 3)
            for h in range(3):
                q_lo_of(h, h)
                split_lo(h, h % 4, PK[:, h, 1, :], PK[:, h, 0, :])
            for g in range(4):
                u_lo(3 + g, (3 + g) % 4, g, 0)
            state_lo(1, 0, 0)
            reduce_tables(1)
            magnitudes(1)

            def output(u, k):
                eng.copy_predicated(x_sb[u][:, 512 * k:512 * (k + 1)], mask[:, 512 * k:512 * (k + 1)],
                                    ps_y[k % 2][:, :]).then_inc(y_out, 1)

            def channel(h, u, last, quad):
                nxt, gen = not last or h + 1 < H, not last or h + 3 < H
                for c in range(NCH):
                    if c in (2, 4):
                        eng.wait_ge(y_ready, h * 4 + (c // 2 + Y_START))
                    if c < NCH - 2:
                        state_lo(h * 7 + (c + 2), c + 1, u % 2)
                    if c in (2, 4):
                        output(u, c // 2 - 1)
                    if c == 0 and gen:
                        q_lo_of(h + 3, (u + 3) % UNROLL)
                    if c < 4 and nxt:
                        u_lo(group(h, c), bank(u, c, h), c, (u + 1) % 2)
                    if c == 4 and gen:
                        split_lo(group(h, 4), bank(u, 4, h), PK[:, (u + 3) % UNROLL, 1, :], PK[:, (u + 3) % UNROLL, 0, :])
                    if c == 5:
                        eng.wait_ge(y_ready, h * 4 + (3 + Y_START))
                        if nxt:
                            state_lo(h * 7 + 8, 0, (u + 1) % 2)
                        output(u, 2)
                    if c == 5 and u == 3 and not last:
                        reduce_tables(quad + 2)
                    if c == 6 and u == 0 and not last:
                        decay_scalars(quad + 1)
                    if c == 7 and u == 3 and not last:
                        magnitudes(quad + 2)
                eng.wait_ge(y_ready, h * 4 + (4 + Y_START))
                eng.memset(waited[:, :], 0.0)
                output(u, 3)

            with eng.Fori(0, QUADS - 1) as q:
                for u in range(UNROLL):
                    channel(q * UNROLL + u, u, False, q)
            for u in range(UNROLL):
                channel(H - UNROLL + u, u, True, None)

        @block.tensor
        def _(eng):
            def product(dst, lhs, rhs, first):
                for i, (a, b) in enumerate(((0, 0), (0, 1), (1, 0))):
                    ins = eng.matmul(dst, lhs[a], rhs[b], start=first and i == 0, stop=i == 2, skip_group_check=True)
                return ins

            eng.wait_ge(consts_ready, 7)
            eng.wait_ge(dve_params, 8)
            for i in range(4):
                eng.transpose(ps_split[0][:, i * H:(i + 1) * H], par_h[:, i, :, :].rearrange("h a n -> h (a n)"),
                              ident[0:H, 0:H]).then_inc(par_transposed, 1)

            def matrices_group(h, r, t, b):
                eng.wait_ge(q_split, h + 1)
                eng.wait_ge(splits, t + 1)
                for j in range(2):
                    eng.transpose(ps_split[b][:, P * j:P * (j + 1)], Wf[:, r, P * j:P * (j + 1)], ident[:, :])
                eng.matmul(ps_split[b][:, CH:2 * CH], sel_re[:, :], Q[:, r, 0, 0:CH], start=True, stop=False, skip_group_check=True)
                eng.matmul(ps_split[b][:, CH:2 * CH], sel_re[:, :], Q[:, r, 1, 0:CH], start=False, stop=True,
                           skip_group_check=True).then_inc(transposed, 1)

            def input_group(g, r, t, b):
                eng.wait_ge(splits, t + 1)
                for j in range(4):
                    J = 4 * g + j
                    ins = eng.transpose(ps_split[b][:, P * j:P * (j + 1)], x_sb[r][:, P * J:P * (J + 1)], ident[:, :])
                ins.then_inc(transposed, 1)

            def project(half, r, ring):
                n = 4 if half == 0 else NCH - 1 - 4
                for par_ in range(2):
                    lhs = [PK[:, r, i, P * par_:P * (par_ + 1)] for i in range(2)]
                    u8 = [U[ring][i][:, 8 * half:8 * half + 8, :].rearrange("p (c two) b -> p c two b", two=2)[:, 0:n, par_, :]
                          for i in range(2)]
                    ins = product(ps_state[half][:, 0:n, :], lhs, u8, par_ == 0)
                return ins

            def decay(c, r, ring):
                return product(ps_state[c // 4][:, c % 4, :], [LAM[:, r, i, :] for i in range(2)],
                               [S[ring][i][:, c - 1, :] for i in range(2)], False)

            eng.wait_ge(act_params, 1)
            for h in range(3):
                matrices_group(h, h, h, h % 4)
            eng.wait_ge(x_loaded[0], 16)
            for g in range(4):
                input_group(g, 0, 3 + g, (3 + g) % 4)
            eng.wait_ge(splits, SPLIT_CREDIT + PRO_GROUPS)
            project(0, 0, 0).then_inc(state_ready, 1)
            project(1, 0, 0).then_inc(y_ready, Y_START)

            def channel(h, u, last, quad):
                ring = u % 2
                nxt, gen = not last or h + 1 < H, not last or h + 3 < H
                eng.wait_ge(t_loaded[u], quad * 32 + 32)
                eng.wait_ge(gen_ready, h * 3 + 3)
                for c in range(NCH):
                    base = (c % 2) * CH
                    yb = ps_y[(c // 2) % 2]
                    if c % 2 == 0:
                        eng.wait_ge(y_out, h * 4 + (c // 2 + 1))
                    for b_, n in ((0, CH), (1, P)):
                        ins = product(yb[:, base + P * b_:base + CH],
                                [U[ring][i][:, 2 * c + b_, :] for i in range(2)],
                                [T[:, u, i, 0:n] for i in range(2)], c % 2 == 0 and b_ == 0)
                    if c < NCH - 1:
                        eng.wait_ge(s_split, h * 7 + (c + 1))
                    if c < NCH - 2:
                        decay(c + 1, u, ring).then_inc(state_ready, 1)
                    if c > 0:
                        ins = product(yb[:, base:base + CH], [S[ring][i][:, c - 1, :] for i in range(2)],
                                [Q[:, u, i, 1:1 + CH] for i in range(2)], False)
                    if c % 2 == 1:
                        ins.then_inc(y_ready, 1)
                    if c < 4 and nxt:
                        if c == 0:
                            eng.wait_ge(x_loaded[(u + 1) % UNROLL], (quad + (u == UNROLL - 1)) * 16 + 16)
                        input_group(c, (u + 1) % UNROLL, group(h, c), bank(u, c, h))
                    if c == 4 and gen:
                        matrices_group(h + 3, (u + 3) % UNROLL, group(h, 4), bank(u, 4, h))
                    if c == 5 and nxt:
                        eng.wait_ge(splits, group(h, 1) + (SPLIT_CREDIT + 1))
                        project(0, (u + 1) % UNROLL, 1 - ring).then_inc(state_ready, 1)
                    if c == 6 and nxt:
                        eng.wait_ge(splits, group(h, 3) + (SPLIT_CREDIT + 1))
                        project(1, (u + 1) % UNROLL, 1 - ring)

            with eng.Fori(0, QUADS - 1) as q:
                for u in range(UNROLL):
                    channel(q * UNROLL + u, u, False, q)
            for u in range(UNROLL):
                channel(H - UNROLL + u, u, True, QUADS - 1)


_INS = ["x", "itok_B_8_3872", "L0_cond_log_dt", "L0_cond_C", "L0_cond_log_A_real", "L0_cond_A_imag", "L0_cond_D"]


def kernel(**inputs):
    import numpy as np
    import concourse.bacc as bacc
    from concourse.bass_utils import run_bass_kernel_spmd

    nc = bacc.Bacc("TRN2", target_bir_lowering=False, num_devices=1)
    arrays, args = {}, []
    for name in _INS:
        a = np.ascontiguousarray(inputs[name])
        arrays[f"in_{name}"] = a
        args.append(nc.dram_tensor(f"in_{name}", a.shape, mybir.dt.from_np(a.dtype), kind="ExternalInput").ap())
    shape = arrays["in_x"].shape
    out = nc.dram_tensor("out_0", shape, F32, kind="ExternalOutput").ap()
    build(nc, *args, out)
    r = run_bass_kernel_spmd(nc, [arrays], core_ids=[0])
    return r.results[0]["out_0"]
```

```python
from contextlib import ExitStack

import concourse.bass as bass
from concourse import mybir

F32 = mybir.dt.float32
F32R = mybir.dt.float32r
I32 = mybir.dt.int32
U8 = mybir.dt.uint8
ALU = mybir.AluOpType
ACT = mybir.ActivationFunctionType

P = 128
CH = 256
PI = 3.14159274101257324
PI_BELOW = 3.1415925
HALF_PI = 1.57079637050628662
INV_2PI = 0.159154943091895336
TWO_PI = (6.28125, 0.0019350051879882812, 3.0199159819567e-07)
MAGIC = 12582912.0
LOG2E = 1.44269504088896341
LN2 = (0.693359375, -2.12194440054690583e-4)
EXP_POLY = (1 / 5040, 1 / 720, 1 / 120, 1 / 24, 1 / 6, 1 / 2, 1.0)

UNROLL = 4
AR = 16
AA = 17
NK = AR + AA
NQ = CH + 1
PRO_GROUPS = 6
SPLIT_CREDIT = 2
PIECES = 5
PAD_WRITES = 32
Y_CREDIT = 4


def build(nc, x, lengths, log_dt, C, log_A_real, A_imag, D, out):
    B, H, L = x.shape
    N = A_imag.shape[1]
    NCH = L // CH
    NB = L // P
    QUADS = H // UNROLL
    HP = H + UNROLL
    assert B == P and N == 64 and H <= P and H % UNROLL == 0 and QUADS >= 2 and NCH == 8

    ctx = ExitStack()
    with ctx:
        def sb(name, shape, dt=F32):
            return ctx.enter_context(nc.sbuf_tensor(name, shape, dt))

        def sem(name):
            return ctx.enter_context(nc.semaphore(name))

        x_sb = [sb(f"x{r}", [P, L]) for r in range(UNROLL)]
        U = [[sb(f"u{r}{p}", [P, NB, P], F32R) for p in ("hi", "lo")] for r in range(UNROLL)]
        ST = sb("state_t", [P, 2, P])
        S = sb("state", [P, 4, 2, P], F32R)
        TPK = sb("toeplitz_proj_k", [P, UNROLL, 2, CH + 512], F32R)
        QL = sb("readout_decay", [P, UNROLL, 2, NQ + P + 1], F32R)
        Wf = sb("powers", [P, 2, CH])
        Qf = sb("readout_f32", [P, 2, AA * AR])
        prod = [sb(f"prod{i}", [P, AA * AR]) for i in range(2)]
        mask = sb("mask", [P, L], U8)
        ident = sb("ident", [P, P])
        sel_re_f = sb("sel_re_f", [P, P])
        sel_re = sb("sel_re", [P, P], F32R)
        fold = sb("fold", [P, N])
        kv = sb("kv", [P, NK])
        half_pi = sb("half_pi", [P, 1])
        minus_re = sb("minus_re", [P, 1])
        zero = sb("zero", [P, 2, P])
        pos = sb("pos", [P, L])
        len_i = sb("len_i", [P, 1], I32)
        len_f = sb("len_f", [P, 1])
        e_in = sb("e_in", [H, 1 + N])
        e_t = [sb(f"e_t{i}", [H, 1 + N]) for i in range(3)]
        e_i = sb("e_i", [H, 1 + N], I32)
        e_out = sb("e_out", [H, 1 + N])
        aim = sb("aim", [H, N])
        c_in = sb("c_in", [H, N, 2])
        par_h = sb("par_h", [H, 4, 2, N])
        pt = [sb(f"pt{i}", [H, N]) for i in range(12)]
        d_in = sb("d_in", [1, H])
        dcol = sb("dcol", [P, HP])
        par = sb("par", [P, 4, HP])
        ang = sb("ang", [P, UNROLL, NK])
        dec = sb("dec", [P, UNROLL, NK])
        turns = sb("turns", [P, UNROLL, NK])
        turns_r = sb("turns_r", [P, UNROLL, NK])
        red = [sb(f"red{i}", [P, UNROLL, NK]) for i in range(4)]
        ared = sb("ared", [P, UNROLL, NK])
        th = sb("th", [P, UNROLL, NK])
        th_u = sb("th_u", [P, UNROLL, NK])
        th_r = sb("th_r", [P, UNROLL, NK])
        mag = sb("mag", [P, UNROLL, NK])
        trig_y = [sb(f"trig_y{i}", [P, UNROLL, AR]) for i in range(2)]
        trig_x = [sb(f"trig_x{i}", [P, UNROLL, AA]) for i in range(2)]
        Y = [sb(f"y_tab{i}", [P, UNROLL, AR]) for i in range(2)]
        X = [sb(f"x_tab{i}", [P, UNROLL, AA]) for i in range(2)]
        XG = [sb(f"xg_tab{i}", [P, UNROLL, AA]) for i in range(2)]
        xprod = [sb(f"xprod{i}", [P, UNROLL, AA]) for i in range(4)]
        lam_f = sb("lam_f", [P, UNROLL, 2])
        lam_s = sb("lam_s", [P, UNROLL, 2, 2], F32R)
        waited = sb("waited", [P, 1])
        warm = sb("warm", [P, 1])
        ps_split = [ctx.enter_context(nc.psum_tensor(f"ps_split{i}", [P, 512], F32)) for i in range(2)]
        ps_state = [ctx.enter_context(nc.psum_tensor(f"ps_state{i}", [P, 512], F32)) for i in range(2)]
        ps_y = [ctx.enter_context(nc.psum_tensor(f"ps_y{i}", [P, 512], F32)) for i in range(4)]
        k_pad = nc.dram_tensor("k_pad", [UNROLL, 2, 2, P + CH], F32, kind="Internal")

        consts_ready = sem("consts_ready")
        params_in = sem("params_in")
        len_in = sem("len_in")
        dve_step = sem("dve_step")
        act_step = sem("act_step")
        act_params = sem("act_params")
        dve_params = sem("dve_params")
        par_transposed = sem("par_transposed")
        par_ready = sem("par_ready")
        mask_consts = sem("mask_consts")
        pool_step = sem("pool_step")
        warmed = sem("warmed")
        args_ready = sem("args_ready")
        angles_reduced = sem("angles_reduced")
        trig_ready = sem("trig_ready")
        mag_ready = sem("mag_ready")
        tables_ready = sem("tables_ready")
        lam_ready = sem("lam_ready")
        gen_ready = sem("gen_ready")
        q_hi = sem("q_hi")
        q_split = sem("q_split")
        transposed = sem("transposed")
        hi_done = sem("hi_done")
        splits = sem("splits")
        copied = sem("copied")
        turned = sem("turned")
        s_hi = sem("s_hi")
        s_split = sem("s_split")
        y_ready = sem("y_ready")
        y_out = sem("y_out")
        k_written = sem("k_written")
        written = sem("written")
        x_loaded = [sem(f"x_loaded{r}") for r in range(UNROLL)]
        t_loaded = [sem(f"t_loaded{r}") for r in range(UNROLL)]

        def first(k):
            return isinstance(k, int) and k == -1

        def final(k):
            return isinstance(k, int) and k == H - 1

        def exists(k, lead):
            return not isinstance(k, int) or k + lead < H

        INPUT_GROUPS = ((0, 1), (2,), (3,), ())

        def y_no(k, d, old):
            if first(k):
                return d
            return k * 8 + (4 + d if final(k) else 4 + 2 * d + (0 if old else 1))

        def copy_no(k, d, old):
            if first(k):
                return d
            if final(k):
                return k * 7 + 4 + d
            return k * 7 + 4 + min(2 * d + (0 if old else 1), 6)

        def turn_no(k, d, old):
            if first(k):
                return d - 1
            if final(k):
                return k * 7 + (4 + d if old else 3)
            return k * 7 + (4 + 2 * d if old else 3 + 2 * d)

        def group_no(k, g):
            return k * 5 + (PRO_GROUPS + 5 + g)

        def table_pieces(k, u, d, q):
            if first(k):
                return range(PIECES) if d == 3 else ()
            return (4 * u + d - 11,) if q is not None and 4 * u + d >= 11 else ()

        def each_step(eng, body):
            body(-1, UNROLL - 1, None)
            with eng.Fori(0, QUADS - 1) as q:
                for u in range(UNROLL):
                    body(q * UNROLL + u, u, q)
            for u in range(UNROLL):
                body(H - UNROLL + u, u, None)

        block = ctx.enter_context(nc.Block())

        @block.sync
        def _(eng):
            eng.dma_start(e_in[:, 0:1], log_dt.rearrange("(h o) -> h o", o=1)).then_inc(params_in, 16)
            eng.dma_start(e_in[:, 1:1 + N], log_A_real[:, :]).then_inc(params_in, 16)
            eng.dma_start(aim[:, :], A_imag[:, :]).then_inc(params_in, 16)
            eng.dma_start(c_in[:, :, :], C[:, :, :]).then_inc(params_in, 16)
            eng.dma_start(d_in[:, :], D.rearrange("(o h) -> o h", o=1)).then_inc(params_in, 16)
            eng.dma_start(len_i[:, :], lengths.rearrange("(b o) -> b o", o=1)).then_inc(len_in, 16)
            for h in range(UNROLL - 1):
                eng.dma_start(x_sb[h][:, :], x[:, h, :]).then_inc(x_loaded[h], 16)
            eng.wait_ge(consts_ready, 1)
            for copy in range(2):
                eng.dma_start(k_pad[:, copy, :, 0:P], zero[0:UNROLL, :, :]).then_inc(written, 16)
            eng.wait_ge(written, PAD_WRITES)

            def toeplitz(h, r, group):
                eng.wait_ge(splits, group + (SPLIT_CREDIT + 1))
                eng.dma_start(k_pad[r, :, :, P:P + CH],
                              TPK[0:2, r, :, CH + 2 * P:].bitcast(F32)).then_inc(k_written, 16)
                eng.wait_ge(k_written, h * 16 + 16)
                row = k_pad[r, :, :, :]
                for i in range(2):
                    skewed = bass.AP(row.tensor, row.offset + (i * (P + CH) + P),
                                     [[2 * (P + CH) - N, 2], [-1, N], [1, CH]])
                    eng.dma_start(T_of(r, i).bitcast(F32), skewed).then_inc(t_loaded[r], 16)

            def T_of(r, i):
                return TPK[:, r, i, 0:CH]

            def channel_of(tensor, h):
                return tensor[:, bass.ds(h, 1), :].rearrange("b o l -> b (o l)")

            for h in range(2):
                toeplitz(h, h, h)

            def step(k, u, q):
                r = (u + 3) % UNROLL
                if exists(k, 3) and not first(k):
                    eng.wait_ge(written, k * 16 + PAD_WRITES)
                    eng.dma_start(x_sb[r][:, :], channel_of(x, k + 3)).then_inc(x_loaded[r], 16)
                if not first(k):
                    eng.wait_ge(y_out, y_no(k, 3, True) + (Y_CREDIT + 1))
                    eng.dma_start(channel_of(out, k), x_sb[u][:, :]).then_inc(written, 16)
                if exists(k, 3):
                    if not first(k):
                        eng.wait_ge(y_ready, k * 8 + 4)
                    toeplitz(k + 3, r, group_no(k, 4))

            each_step(eng, step)
            eng.wait_ge(written, H * 16 + PAD_WRITES)

        @block.gpsimd
        def _(eng):
            eng.memset(zero[:, :, :], 0.0).then_inc(consts_ready, 1)
            eng.memset(ident[:, :], 1.0).then_inc(pool_step, 1)
            eng.memset(sel_re_f[:, :], 1.0).then_inc(pool_step, 1)
            eng.memset(minus_re[:, :], 1.0).then_inc(pool_step, 1)
            eng.wait_ge(pool_step, 3)
            eng.affine_select(ident[:, :], ident[:, :], [[-1, P]], ALU.is_equal, 0.0, base=0,
                              channel_multiplier=1).then_inc(consts_ready, 1)
            eng.affine_select(sel_re_f[:, :], sel_re_f[:, :], [[0, P]], ALU.is_ge, 0.0, base=N - 1,
                              channel_multiplier=-1).then_inc(consts_ready, 1)
            eng.affine_select(minus_re[:, :], minus_re[:, :], [[0, 1]], ALU.is_ge, -1.0, base=-N,
                              channel_multiplier=1).then_inc(consts_ready, 1)
            eng.iota(kv[:, 0:AR], [[1, AR]], base=0, channel_multiplier=0,
                     allow_small_or_imprecise_dtypes=True).then_inc(consts_ready, 1)
            eng.iota(kv[:, AR:NK], [[AR, AA]], base=0, channel_multiplier=0,
                     allow_small_or_imprecise_dtypes=True).then_inc(consts_ready, 1)
            eng.memset(half_pi[:, :], HALF_PI).then_inc(consts_ready, 1)
            eng.iota(pos[:, :], [[1, L]], base=0, channel_multiplier=0,
                     allow_small_or_imprecise_dtypes=True).then_inc(mask_consts, 1)
            eng.wait_ge(consts_ready, 7)
            eng.tensor_tensor(fold[:, :], ident[:, 0:N], ident[:, N:P], ALU.add).then_inc(pool_step, 1)
            eng.wait_ge(pool_step, 4)

            def times(out_, a, b):
                return eng.tensor_tensor(out_, a, b, ALU.mult)

            def arguments(quad):
                cols = bass.ds(quad * UNROLL, UNROLL)
                k = kv[:, :].unsqueeze(1).broadcast_to([P, UNROLL, NK])
                times(ang[:, :, :], par[:, 1, cols].unsqueeze(2).broadcast_to([P, UNROLL, NK]), k).then_inc(args_ready, 1)
                times(dec[:, :, :], par[:, 0, cols].unsqueeze(2).broadcast_to([P, UNROLL, NK]), k).then_inc(args_ready, 1)

            def tables(quad, done):
                cols = bass.ds(quad * UNROLL, UNROLL)
                eng.wait_ge(trig_ready, done * 7 + 7)
                eng.wait_ge(mag_ready, done + 1)
                if isinstance(done, int) and done == 0:
                    pass
                else:
                    eng.wait_ge(lam_ready, done * 2)
                for i in range(2):
                    times(Y[i][:, :, :], trig_y[i][:, :, :], mag[:, :, 0:AR]).then_inc(pool_step, 1)
                    times(X[i][:, :, :], trig_x[i][:, :, :], mag[:, :, AR:NK]).then_inc(pool_step, 1)
                eng.wait_ge(pool_step, done * 8 + 8)
                g1 = par[:, 2, cols].unsqueeze(2).broadcast_to([P, UNROLL, AA])
                g2 = par[:, 3, cols].unsqueeze(2).broadcast_to([P, UNROLL, AA])
                times(xprod[0][:, :, :], X[0][:, :, :], g1).then_inc(pool_step, 1)
                times(xprod[1][:, :, :], X[1][:, :, :], g2).then_inc(pool_step, 1)
                times(xprod[2][:, :, :], X[1][:, :, :], g1).then_inc(pool_step, 1)
                times(xprod[3][:, :, :], X[0][:, :, :], g2).then_inc(pool_step, 1)
                eng.wait_ge(pool_step, done * 8 + 12)
                eng.tensor_tensor(XG[0][:, :, :], xprod[0][:, :, :], xprod[1][:, :, :], ALU.add).then_inc(tables_ready, 1)
                eng.tensor_tensor(XG[1][:, :, :], xprod[2][:, :, :], xprod[3][:, :, :], ALU.subtract).then_inc(tables_ready, 1)
                eng.wait_ge(tables_ready, done * 2 + 2)

            gen_step = sem("gen_step")

            def matrices(h, r, quad_no, uses_before):
                def outer(dst, hi, n, step):
                    hi_b = [hi[i][:, r, 0:n].unsqueeze(2).broadcast_to([P, n, AR]) for i in range(2)]
                    lo_b = [Y[i][:, r, :].unsqueeze(1).broadcast_to([P, n, AR]) for i in range(2)]
                    for i in range(2):
                        times(prod[i][:, 0:n * AR].rearrange("p (a r) -> p a r", r=AR), hi_b[i], lo_b[i]).then_inc(gen_step, 1)
                    eng.wait_ge(gen_step, h * 6 + (step + 2))
                    return eng.tensor_tensor(dst, prod[0][:, 0:n * AR], prod[1][:, 0:n * AR], ALU.add).then_inc(gen_step, 1)
                forward = Wf[:, r % 2, :]
                backward = bass.AP(forward.tensor, forward.offset + (CH - 1), [list(forward.ap[0]), [-1, CH]])
                outer(backward, X, AA - 1, 0)
                eng.wait_ge(gen_step, h * 6 + 3)
                outer(Qf[:, r % 2, :], XG, AA, 3)
                eng.wait_ge(gen_step, h * 6 + 6)
                eng.tensor_tensor(Qf[:, r % 2, 0:1], Qf[:, r % 2, 0:1], dcol[:, bass.ds(h, 1)], ALU.add).then_inc(gen_ready, 1)
                eng.wait_ge(lam_ready, quad_no * 2 + 2)
                if uses_before is not None:
                    eng.wait_ge(y_ready, uses_before)
                v = lam_s[:, r, :, :].bitcast(F32).unsqueeze(3).broadcast_to([P, 2, 2, N])
                m = fold[:, :].unsqueeze(1).broadcast_to([P, 2, N])
                for i in range(2):
                    times(QL[:, r, i, NQ:NQ + P].rearrange("p (a m) -> p a m", a=2), m, v[:, i, :, :]).then_inc(gen_ready, 1)

            eng.wait_ge(par_ready, 3)
            arguments(0)
            tables(0, 0)
            for h in range(2):
                matrices(h, h, 0, None)

            def step(k, u, q):
                if exists(k, 3):
                    if not first(k):
                        eng.wait_ge(splits, group_no(k - 2, 4) + (SPLIT_CREDIT + 1))
                    else:
                        eng.wait_ge(splits, SPLIT_CREDIT + 1)
                    quad = 0 if first(k) else QUADS - 1 if q is None else q if u == 0 else q + 1
                    matrices(k + 3, (u + 3) % UNROLL, quad, None if first(k) else k * 8 + 4)
                if first(k) or (u == 2 and q is not None):
                    arguments(1 if first(k) else q + 2)
                if u == 0 and q is not None:
                    tables(q + 1, q + 1)

            each_step(eng, step)

        @block.scalar
        def _(eng):
            def angle_tables(done, piece):
                def cos(dst, rows, ks):
                    eng.activation(dst[rows, :, :], ared[rows, :, ks], ACT.Sin, bias=half_pi[rows, :], scale=-1.0).then_inc(trig_ready, 1)
                def sin(dst, rows, ks, scale):
                    eng.activation(dst[rows, :, :], red[3][rows, :, ks], ACT.Sin, scale=scale).then_inc(trig_ready, 1)
                re, im, low, high = slice(0, N), slice(N, P), slice(0, AR), slice(AR, NK)
                if piece == 0:
                    eng.wait_ge(args_ready, done * 2 + 2)
                    eng.activation(th[:, :, :], dec[:, :, :], ACT.Tanh, scale=0.5).then_inc(trig_ready, 1)
                elif piece == 3:
                    eng.wait_ge(angles_reduced, done + 1)
                    eng.activation(ared[:, :, :], red[3][:, :, :], ACT.Abs).then_inc(act_step, 1)
                    sin(trig_y[0], im, low, 1.0)
                    sin(trig_y[1], re, low, 1.0)
                    sin(trig_x[1], slice(0, P), high, minus_re[:, 0:1])
                elif piece == 4:
                    eng.wait_ge(act_step, done + 1)
                    cos(trig_y[0], re, low)
                    cos(trig_y[1], im, low)
                    cos(trig_x[0], slice(0, P), high)

            eng.wait_ge(consts_ready, 7)
            eng.activation(warm[:, :], half_pi[:, :], ACT.Silu).then_inc(warmed, 1)
            eng.activation(sel_re[:, :], sel_re_f[:, :], ACT.Copy).then_inc(act_params, 1)
            eng.wait_ge(dve_params, 1)
            eng.activation(pt[0][:, :], par_h[:, 0, 0, :], ACT.Tanh, scale=0.5).then_inc(act_params, 1)
            eng.wait_ge(dve_params, 2)
            eng.activation(pt[4][:, :], pt[3][:, :], ACT.Abs).then_inc(act_params, 1)
            eng.activation(pt[5][:, :], pt[3][:, :], ACT.Sin).then_inc(act_params, 1)
            eng.activation(pt[6][:, :], pt[3][:, :], ACT.Sin, scale=0.5).then_inc(act_params, 1)
            eng.wait_ge(act_params, 3)
            eng.activation(pt[7][:, :], pt[4][:, :], ACT.Sin, bias=half_pi[0:H, :], scale=-1.0).then_inc(act_params, 1)
            for piece in range(PIECES):
                angle_tables(0, piece)

            def split_hi(t, b, dst):
                eng.wait_ge(transposed, t + 1)
                eng.activation(dst, ps_split[b][:, :], ACT.Copy).then_inc(hi_done, 1)

            def q_hi_of(h, r):
                eng.wait_ge(gen_ready, h * 3 + 1)
                eng.activation(QL[:, r, 0, 0:NQ], Qf[:, r % 2, 0:NQ], ACT.Copy).then_inc(q_hi, 1)

            def u_hi(g, r):
                return U[r][0][:, 4 * g:4 * g + 4, :].rearrange("p j b -> p (j b)")

            for h in range(2):
                q_hi_of(h, h)
                split_hi(h, h % 2, TPK[:, h, 0, CH:])
            for g in range(4):
                split_hi(2 + g, g % 2, u_hi(g, 0))

            def step(k, u, q):
                pk = k if q is None else u

                def state_copy(d, old):
                    eng.wait_ge(y_ready, y_no(k, d, old) + 1)
                    eng.activation(ST[:, copy_no(pk, d, old) % 2, :], ps_y[y_no(pk, d, old) % 4][:, CH:CH + P],
                                   ACT.Copy).then_inc(copied, 1)

                def state_hi(d, old):
                    n, pn = turn_no(k, d, old), turn_no(pk, d, old)
                    eng.wait_ge(turned, n + 1)
                    eng.activation(S[:, pn % 4, 0, :], ps_state[pn % 2][:, 0:P], ACT.Copy).then_inc(s_hi, 1)

                if not first(k):
                    eng.wait_ge(y_ready, k * 8 + 4)
                for d in range(4):
                    if not (first(k) and d == 0) and not (final(k) and d > 0):
                        state_hi(d, False)
                    if d > 0 and not first(k) and d < 3:
                        state_copy(d, True)
                    if exists(k, 2):
                        for g in INPUT_GROUPS[d]:
                            split_hi(group_no(k, g), group_no(pk, g) % 2, u_hi(g, (u + 2) % UNROLL))
                    if d == 0 and not first(k):
                        state_copy(d, True)
                    if d == 3 and exists(k, 3):
                        split_hi(group_no(k, 4), group_no(pk, 4) % 2, TPK[:, (u + 3) % UNROLL, 0, CH:])
                    if not first(k) and d < 3:
                        state_hi(d, True)
                    if not final(k):
                        state_copy(d, False)
                    if d == 1 and exists(k, 3):
                        q_hi_of(k + 3, (u + 3) % UNROLL)
                    for piece in table_pieces(k, u, d, q):
                        angle_tables(1 if first(k) else q + 2, piece)

            each_step(eng, step)

        @block.vector
        def _(eng):
            count = [0]

            def step(ins):
                count[0] += 1
                ins.then_inc(dve_step, 1)
                eng.wait_ge(dve_step, count[0])

            def reduce_angle(i, ang_, t0, t1, r):
                if i == 0:
                    return eng.tensor_scalar(t0, ang_, INV_2PI, MAGIC, ALU.mult, ALU.add)
                if i == 1:
                    return eng.tensor_scalar(t1, t0, MAGIC, None, ALU.subtract)
                if i < 5:
                    return eng.scalar_tensor_tensor(r[i - 2], t1, -TWO_PI[i - 2], ang_ if i == 2 else r[i - 3], ALU.mult, ALU.add)
                return eng.tensor_scalar(r[3], r[2], PI_BELOW, -PI_BELOW, ALU.min, ALU.max)

            eng.memset(dcol[:, :], 0.0).then_inc(dve_step, 1)
            eng.memset(par[:, :, :], 0.0).then_inc(dve_step, 1)
            count[0] = 2
            eng.wait_ge(params_in, 80)
            e, f, n_ = (t[:, :] for t in e_t)
            step(eng.tensor_scalar(e_in[:, :], e_in[:, :], 88.0, -87.0, ALU.min, ALU.max))
            step(eng.tensor_scalar(f, e_in[:, :], LOG2E, MAGIC, ALU.mult, ALU.add))
            step(eng.tensor_scalar(n_, f, MAGIC, None, ALU.subtract))
            step(eng.scalar_tensor_tensor(e, n_, -LN2[0], e_in[:, :], ALU.mult, ALU.add))
            step(eng.scalar_tensor_tensor(e_in[:, :], n_, -LN2[1], e, ALU.mult, ALU.add))
            step(eng.tensor_scalar(f, e_in[:, :], EXP_POLY[0], None, ALU.mult))
            for a in EXP_POLY[1:]:
                step(eng.scalar_tensor_tensor(f, f, a, e_in[:, :], ALU.add, ALU.mult))
            step(eng.tensor_scalar(f, f, 1.0, None, ALU.add))
            step(eng.tensor_scalar(n_, n_, 127.0, 8388608.0, ALU.add, ALU.mult))
            step(eng.tensor_copy(e_i[:, :], n_))
            step(eng.tensor_tensor(e_out[:, :], f, e_i[:, :].bitcast(F32), ALU.mult))
            dt, aexp = e_out[:, 0:1], e_out[:, 1:1 + N]
            p = [t[:, :] for t in pt]
            step(eng.tensor_scalar(p[8], aexp, -1.0, None, ALU.mult))
            step(eng.tensor_scalar(par_h[:, 1, 0, :], aim[:, :], dt, None, ALU.mult))
            eng.tensor_scalar(par_h[:, 0, 0, :], p[8], dt, None, ALU.mult).then_inc(dve_params, 1)
            for i in range(5):
                step(reduce_angle(i, par_h[:, 1, 0, :], p[1], p[2], [p[9], p[10], p[11], p[3]]))
            reduce_angle(5, par_h[:, 1, 0, :], p[1], p[2], [p[9], p[10], p[11], p[3]]).then_inc(dve_params, 1)
            eng.wait_ge(act_params, 6)
            step(eng.tensor_scalar(p[1], p[0], -1.0, 1.0, ALU.mult, ALU.add))
            step(eng.reciprocal(p[2], p[1]))
            step(eng.scalar_tensor_tensor(p[1], p[0], 2.0, p[2], ALU.mult, ALU.mult))
            step(eng.scalar_tensor_tensor(p[2], p[1], 1.0, p[5], ALU.add, ALU.mult))
            step(eng.tensor_tensor(p[1], p[1], p[7], ALU.mult))
            step(eng.scalar_tensor_tensor(p[3], p[6], -2.0, p[6], ALU.mult, ALU.mult))
            step(eng.tensor_tensor(p[1], p[1], p[3], ALU.add))
            step(eng.tensor_tensor(p[5], p[8], p[8], ALU.mult))
            step(eng.tensor_tensor(p[6], aim[:, :], aim[:, :], ALU.mult))
            step(eng.tensor_tensor(p[5], p[5], p[6], ALU.add))
            step(eng.reciprocal(p[7], p[5]))
            step(eng.tensor_tensor(p[3], p[1], p[8], ALU.mult))
            step(eng.tensor_tensor(p[4], p[2], aim[:, :], ALU.mult))
            step(eng.tensor_tensor(p[3], p[3], p[4], ALU.add))
            step(eng.tensor_tensor(p[3], p[3], p[7], ALU.mult))
            step(eng.tensor_tensor(p[5], p[2], p[8], ALU.mult))
            step(eng.tensor_tensor(p[6], p[1], aim[:, :], ALU.mult))
            step(eng.tensor_tensor(p[5], p[5], p[6], ALU.subtract))
            step(eng.tensor_tensor(p[4], p[5], p[7], ALU.mult))
            cre, cim = c_in[:, :, 0:1].rearrange("h n o -> h (n o)"), c_in[:, :, 1:2].rearrange("h n o -> h (n o)")
            step(eng.tensor_tensor(p[5], cre, p[3], ALU.mult))
            step(eng.tensor_tensor(p[6], cim, p[4], ALU.mult))
            step(eng.tensor_tensor(p[5], p[5], p[6], ALU.subtract))
            step(eng.tensor_tensor(p[9], cre, p[4], ALU.mult))
            step(eng.tensor_tensor(p[10], cim, p[3], ALU.mult))
            step(eng.tensor_tensor(p[9], p[9], p[10], ALU.add))
            eng.tensor_scalar(par_h[:, 2, 0, :], p[5], 2.0, None, ALU.mult).then_inc(dve_params, 1)
            eng.tensor_scalar(par_h[:, 2, 1, :], p[5], -2.0, None, ALU.mult).then_inc(dve_params, 1)
            for half in range(2):
                eng.tensor_scalar(par_h[:, 3, half, :], p[9], 2.0, None, ALU.mult).then_inc(dve_params, 1)
            for i in range(2):
                eng.tensor_copy(par_h[:, i, 1, :], par_h[:, i, 0, :]).then_inc(dve_params, 1)
            eng.tensor_scalar(dcol[0:1, 0:H], d_in[:, :], 1.0, None, ALU.add).then_inc(par_ready, 1)
            eng.wait_ge(par_transposed, 4)
            eng.tensor_copy(par[:, :, 0:H], ps_split[0][:, 0:4 * H].rearrange("p (i h) -> p i h", i=4)).then_inc(par_ready, 2)
            eng.wait_ge(par_ready, 3)
            eng.memset(th_u[:, 0, 0:1], 0.0).then_inc(splits, SPLIT_CREDIT)
            eng.memset(th_u[:, 0, 1:2], 0.0).then_inc(y_out, Y_CREDIT)

            tab_step = sem("tab_step")

            def reduce_and_magnitudes(done, piece):
                if piece < 3:
                    if piece == 0:
                        eng.wait_ge(args_ready, done * 2 + 2)
                    for i in (2 * piece, 2 * piece + 1):
                        if i > 0:
                            eng.wait_ge(tab_step, done * 8 + i)
                        ins = reduce_angle(i, ang[:, :, :], turns[:, :, :], turns_r[:, :, :], [r[:, :, :] for r in red])
                        ins.then_inc(angles_reduced if i == 5 else tab_step, 1)
                    return
                if piece == 3:
                    eng.wait_ge(trig_ready, done * 7 + 1)
                    eng.tensor_scalar(th_u[:, :, :], th[:, :, :], -1.0, 1.0, ALU.mult, ALU.add).then_inc(tab_step, 1)
                    eng.wait_ge(tab_step, done * 8 + 6)
                    eng.reciprocal(th_r[:, :, 0:AR], th_u[:, :, 0:AR]).then_inc(tab_step, 1)
                else:
                    eng.reciprocal(th_r[:, :, AR:NK], th_u[:, :, AR:NK]).then_inc(tab_step, 1)
                    eng.wait_ge(tab_step, done * 8 + 8)
                    eng.scalar_tensor_tensor(mag[:, :, :], th[:, :, :], 1.0, th_r[:, :, :], ALU.add, ALU.mult).then_inc(mag_ready, 1)

            lam_step = sem("lam_step")

            def decay_scalars(done):
                eng.wait_ge(tables_ready, done * 2 + 2)
                if not (isinstance(done, int) and done == 0):
                    eng.wait_ge(gen_ready, done * 12)
                re, im, k256 = slice(0, N), slice(N, P), slice(AA - 1, AA)
                eng.tensor_copy(lam_f[re, :, 0:1], X[0][re, :, k256]).then_inc(lam_step, 1)
                eng.tensor_scalar(lam_f[im, :, 0:1], X[1][im, :, k256], -1.0, None, ALU.mult).then_inc(lam_step, 1)
                eng.tensor_scalar(lam_f[re, :, 1:2], X[1][re, :, k256], -1.0, None, ALU.mult).then_inc(lam_step, 1)
                eng.tensor_copy(lam_f[im, :, 1:2], X[0][im, :, k256]).then_inc(lam_step, 1)
                eng.wait_ge(lam_step, done * 4 + 4)
                eng.tensor_copy(lam_s[:, :, 0, :], lam_f[:, :, :]).then_inc(lam_ready, 1)
                eng.wait_ge(lam_ready, done * 2 + 1)
                eng.tensor_tensor(lam_s[:, :, 1, :], lam_f[:, :, :], lam_s[:, :, 0, :].bitcast(F32), ALU.subtract).then_inc(lam_ready, 1)

            def split_lo(t, b, dst, hi):
                eng.wait_ge(hi_done, t + 1)
                eng.tensor_tensor(dst, ps_split[b][:, :], hi.bitcast(F32), ALU.subtract).then_inc(splits, 1)

            def q_lo_of(h, r):
                eng.wait_ge(q_hi, h + 1)
                eng.tensor_tensor(QL[:, r, 1, 0:NQ], Qf[:, r % 2, 0:NQ], QL[:, r, 0, 0:NQ].bitcast(F32),
                                  ALU.subtract).then_inc(q_split, 1)

            def matrices_lo(t, b, r):
                split_lo(t, b, TPK[:, r, 1, CH:], TPK[:, r, 0, CH:])

            def u_lo(t, b, g, r):
                hi, lo = (U[r][i][:, 4 * g:4 * g + 4, :].rearrange("p j b -> p (j b)") for i in range(2))
                split_lo(t, b, lo, hi)

            for piece in range(PIECES):
                reduce_and_magnitudes(0, piece)
            decay_scalars(0)
            eng.wait_ge(len_in, 16)
            eng.wait_ge(mask_consts, 1)
            eng.tensor_copy(len_f[:, :], len_i[:, :]).then_inc(mask_consts, 1)
            eng.wait_ge(mask_consts, 2)
            eng.tensor_scalar(mask[:, :], pos[:, :], len_f[:, 0:1], None, ALU.is_lt).then_inc(mask_consts, 1)
            eng.wait_ge(mask_consts, 3)
            for h in range(2):
                q_lo_of(h, h)
                matrices_lo(h, h % 2, h)
            for g in range(4):
                u_lo(2 + g, g % 2, g, 0)

            def step(k, u, q):
                pk = k if q is None else u

                def state_lo(d, old):
                    n, pn = turn_no(k, d, old), turn_no(pk, d, old)
                    eng.wait_ge(s_hi, n + 1)
                    eng.tensor_tensor(S[:, pn % 4, 1, :], ps_state[pn % 2][:, 0:P], S[:, pn % 4, 0, :].bitcast(F32),
                                      ALU.subtract).then_inc(s_split, 1)

                def output(channel_place, c, number):
                    cols = slice(CH * c, CH * (c + 1))
                    eng.copy_predicated(x_sb[channel_place][:, cols], mask[:, cols], ps_y[number % 4][:, 0:CH]).then_inc(y_out, 1)

                for d in range(4):
                    if not (first(k) and d == 0) and not (final(k) and d > 0):
                        state_lo(d, False)
                        if d == 0:
                            output(u, 3, 3)
                        else:
                            output((u + 1) % UNROLL, d - 1, y_no(pk, d - 1, False))
                    if exists(k, 2):
                        for g in INPUT_GROUPS[d]:
                            u_lo(group_no(k, g), group_no(pk, g) % 2, g, (u + 2) % UNROLL)
                    if not first(k) and d < 3:
                        state_lo(d, True)
                        output(u, 4 + d, y_no(pk, d, True))
                    if d == 1 and exists(k, 3):
                        q_lo_of(k + 3, (u + 3) % UNROLL)
                    if d == 3 and u == 0 and q is not None:
                        decay_scalars(q + 1)
                    if d == 3 and exists(k, 3):
                        matrices_lo(group_no(k, 4), group_no(pk, 4) % 2, (u + 3) % UNROLL)
                    for piece in table_pieces(k, u, d, q):
                        reduce_and_magnitudes(1 if first(k) else q + 2, piece)
                if not first(k):
                    eng.wait_ge(y_ready, y_no(k, 3, True) + 1)
                    eng.memset(waited[:, :], 0.0)
                    output(u, 7, y_no(pk, 3, True))

            each_step(eng, step)

        @block.tensor
        def _(eng):
            def product(dst, lhs, rhs, first):
                for i, (a, b) in enumerate(((0, 0), (0, 1), (1, 0))):
                    ins = eng.matmul(dst, lhs[a], rhs[b], start=first and i == 0, stop=i == 2, skip_group_check=True)
                return ins

            eng.wait_ge(consts_ready, 7)
            eng.wait_ge(dve_params, 8)
            for i in range(4):
                eng.transpose(ps_split[0][:, i * H:(i + 1) * H], par_h[:, i, :, :].rearrange("h a n -> h (a n)"),
                              ident[0:H, 0:H]).then_inc(par_transposed, 1)

            def matrices_group(h, r, t, b):
                eng.wait_ge(q_split, h + 1)
                eng.wait_ge(splits, t + 1)
                for j in range(2):
                    eng.transpose(ps_split[b][:, P * j:P * (j + 1)], Wf[:, r % 2, P * j:P * (j + 1)], ident[:, :])
                eng.matmul(ps_split[b][:, CH:2 * CH], sel_re[:, :], QL[:, r, 0, 0:CH], start=True, stop=False, skip_group_check=True)
                eng.matmul(ps_split[b][:, CH:2 * CH], sel_re[:, :], QL[:, r, 1, 0:CH], start=False, stop=True,
                           skip_group_check=True).then_inc(transposed, 1)

            def input_group(g, r, t, b):
                eng.wait_ge(splits, t + 1)
                for j in range(4):
                    J = 4 * g + j
                    ins = eng.transpose(ps_split[b][:, P * j:P * (j + 1)], x_sb[r][:, P * J:P * (J + 1)], ident[:, :])
                ins.then_inc(transposed, 1)

            def inputs_product(bank, r, c):
                states = c < NCH - 1
                n = CH + P if states else CH
                product(bank[:, 0:n], [U[r][i][:, 2 * c, :] for i in range(2)],
                        [TPK[:, r, i, 0:n] for i in range(2)], True)
                if states:
                    rhs = [TPK[:, r, i, 0:CH + 2 * P].rearrange("p (a n) -> p a n", n=P)[:, 0:4:3, :] for i in range(2)]
                    dst = bank[:, P:P + CH].rearrange("p (a n) -> p a n", n=P)
                else:
                    rhs, dst = [TPK[:, r, i, 0:P] for i in range(2)], bank[:, P:CH]
                return product(dst, [U[r][i][:, 2 * c + 1, :] for i in range(2)], rhs, False)

            def state_product(bank, place, r, c):
                n = CH + P if c < NCH - 1 else CH
                return product(bank[:, 0:n], [S[:, place, i, :] for i in range(2)],
                               [QL[:, r, i, 1:1 + n] for i in range(2)], False)

            eng.wait_ge(act_params, 1)
            for h in range(2):
                matrices_group(h, h, h, h % 2)
            eng.wait_ge(x_loaded[0], 16)
            for g in range(4):
                input_group(g, 0, 2 + g, g % 2)

            def step(k, u, q):
                pk = k if q is None else u
                quad = QUADS - 1 if q is None else q

                def turn(d, old):
                    n, pn = turn_no(k, d, old), turn_no(pk, d, old)
                    eng.wait_ge(copied, n + 1)
                    if not (isinstance(n, int) and n < 2):
                        eng.wait_ge(s_split, n - 1)
                    eng.transpose(ps_state[pn % 2][:, 0:P], ST[:, pn % 2, :], ident[:, :]).then_inc(turned, 1)

                def begin(d, old):
                    n, pn = y_no(k, d, old), y_no(pk, d, old)
                    c, r = (4 + d, u) if old else (d, (u + 1) % UNROLL)
                    eng.wait_ge(y_out, n + 1)
                    return inputs_product(ps_y[pn % 4], r, c)

                def complete(d, old):
                    pn = y_no(pk, d, old)
                    c, r = (4 + d, u) if old else (d, (u + 1) % UNROLL)
                    m, pm = (turn_no(j, d - 1 if old and d > 0 else d, old and d > 0) for j in (k, pk))
                    eng.wait_ge(s_split, m + 1)
                    state_product(ps_y[pn % 4], pm % 4, r, c).then_inc(y_ready, 1)

                if not final(k):
                    eng.wait_ge(splits, (PRO_GROUPS if first(k) else group_no(k - 1, 3) + 1) + SPLIT_CREDIT)
                    eng.wait_ge(t_loaded[(u + 1) % UNROLL], 32 if first(k) else (quad + (u == 3)) * 32 + 32)
                    eng.wait_ge(gen_ready, k * 3 + 6)
                if exists(k, 2):
                    eng.wait_ge(x_loaded[(u + 2) % UNROLL], 16 if first(k) else (quad + (u >= 2)) * 16 + 16)
                def input_groups(d):
                    if exists(k, 2):
                        for g in INPUT_GROUPS[d]:
                            input_group(g, (u + 2) % UNROLL, group_no(k, g), group_no(pk, g) % 2)

                for d in range(4):
                    if not first(k):
                        begin(d, True)
                    if d == 0:
                        if not first(k):
                            turn(d, False)
                        input_groups(d)
                        if not first(k):
                            complete(d, True)
                    else:
                        if first(k):
                            input_groups(d)
                        if not final(k):
                            turn(d, False)
                        if not first(k):
                            complete(d, True)
                            input_groups(d)
                    if d == 3 and exists(k, 3):
                        matrices_group(k + 3, (u + 3) % UNROLL, group_no(k, 4), group_no(pk, 4) % 2)
                    if not final(k):
                        ins = begin(d, False)
                        if d == 0:
                            ins.then_inc(y_ready, 1)
                    if not first(k) and d < 3:
                        turn(d, True)
                    if not final(k) and d > 0:
                        complete(d, False)

            each_step(eng, step)


_INS = ["x", "itok_B_8_3872", "L0_cond_log_dt", "L0_cond_C", "L0_cond_log_A_real", "L0_cond_A_imag", "L0_cond_D"]


def kernel(**inputs):
    import numpy as np
    import concourse.bacc as bacc
    from concourse.bass_utils import run_bass_kernel_spmd

    nc = bacc.Bacc("TRN2", target_bir_lowering=False, num_devices=1)
    arrays, args = {}, []
    for name in _INS:
        a = np.ascontiguousarray(inputs[name])
        arrays[f"in_{name}"] = a
        args.append(nc.dram_tensor(f"in_{name}", a.shape, mybir.dt.from_np(a.dtype), kind="ExternalInput").ap())
    shape = arrays["in_x"].shape
    out = nc.dram_tensor("out_0", shape, F32, kind="ExternalOutput").ap()
    build(nc, *args, out)
    r = run_bass_kernel_spmd(nc, [arrays], core_ids=[0])
    return r.results[0]["out_0"]
```

```python
from contextlib import ExitStack

import concourse.bass as bass
from concourse import mybir

F32 = mybir.dt.float32
F32R = mybir.dt.float32r
I32 = mybir.dt.int32
U8 = mybir.dt.uint8
ALU = mybir.AluOpType
ACT = mybir.ActivationFunctionType

P = 128
CH = 256
PI_BELOW = 3.1415925
HALF_PI = 1.57079637050628662
INV_2PI = 0.159154943091895336
TWO_PI = (6.28125, 0.0019350051879882812, 3.0199159819567e-07)
MAGIC = 12582912.0
LOG2E = 1.44269504088896341
LN2 = (0.693359375, -2.12194440054690583e-4)
EXP_POLY = (1 / 5040, 1 / 720, 1 / 120, 1 / 24, 1 / 6, 1 / 2, 1.0)

UNROLL = 4
AR = 16
AA = 17
NK = AR + AA
NQ = CH + 1
PRO_GROUPS = 6
SPLIT_CREDIT = 2
PIECES = 5
PAR_DTA = 2
PAR_ALL = 4
TABLE_SLOTS = ((0,), (1,), (2,), (3, 4))
LAST_STORES = 3
PAD_WRITES = 32
Y_CREDIT = 4


def build(nc, x, lengths, log_dt, C, log_A_real, A_imag, D, out):
    B, H, L = x.shape
    N = A_imag.shape[1]
    NCH = L // CH
    NB = L // P
    QUADS = H // UNROLL
    HP = H + UNROLL
    assert B == P and N == 64 and H <= P and H % UNROLL == 0 and QUADS >= 2 and NCH == 8

    ctx = ExitStack()
    with ctx:
        def sb(name, shape, dt=F32):
            return ctx.enter_context(nc.sbuf_tensor(name, shape, dt))

        def sem(name):
            return ctx.enter_context(nc.semaphore(name))

        x_sb = [sb(f"x{r}", [P, L]) for r in range(UNROLL)]
        U = [[sb(f"u{r}{p}", [P, NB, P], F32R) for p in ("hi", "lo")] for r in range(UNROLL)]
        UF = sb("u_f32", [P, 2, 512])
        ST = sb("state_t", [P, 2, P])
        S = sb("state", [P, 4, 2, P], F32R)
        TPK = sb("toeplitz_proj_k", [P, UNROLL, 2, CH + 512], F32R)
        QL = sb("readout_decay", [P, UNROLL, 2, NQ + P + 1], F32R)
        QK = sb("readout_real", [P, 2, CH], F32R)
        Wf = sb("powers", [P, 2, CH])
        Qf = sb("readout_f32", [P, 2, AA * AR])
        prod = [sb(f"prod{i}", [P, AA * AR]) for i in range(2)]
        dve_prod = [sb(f"dve_prod{i}", [P, AA * AR]) for i in range(2)]
        mask = sb("mask", [P, L], U8)
        ident = sb("ident", [P, P])
        ones_f = sb("ones_f", [P, P])
        ones = sb("ones", [P, P], F32R)
        fold = sb("fold", [P, N])
        kv = sb("kv", [P, NK])
        half_pi = sb("half_pi", [P, 1])
        minus_re = sb("minus_re", [P, 1])
        zero = sb("zero", [P, 2, P])
        pos = sb("pos", [P, L])
        len_i = sb("len_i", [P, 1], I32)
        len_f = sb("len_f", [P, 1])
        e_in = sb("e_in", [H, 1 + N])
        e_t = [sb(f"e_t{i}", [H, 1 + N]) for i in range(3)]
        e_i = sb("e_i", [H, 1 + N], I32)
        e_out = sb("e_out", [H, 1 + N])
        aim = sb("aim", [H, N])
        c_in = sb("c_in", [H, N, 2])
        par_h = sb("par_h", [H, 4, 2, N])
        pt = [sb(f"pt{i}", [H, N]) for i in range(12)]
        pair = [sb(f"pair{i}", [H, 2, N]) for i in range(7)]
        d_in = sb("d_in", [1, H])
        dcol = sb("dcol", [P, HP])
        par = sb("par", [P, 4, HP])
        ang = sb("ang", [P, UNROLL, NK])
        dec = sb("dec", [P, UNROLL, NK])
        turns = sb("turns", [P, UNROLL, NK])
        turns_r = sb("turns_r", [P, UNROLL, NK])
        red = [sb(f"red{i}", [P, UNROLL, NK]) for i in range(4)]
        ared = sb("ared", [P, UNROLL, NK])
        th = sb("th", [P, UNROLL, NK])
        th_u = sb("th_u", [P, UNROLL, NK])
        th_r = sb("th_r", [P, UNROLL, NK])
        mag = sb("mag", [P, UNROLL, NK])
        trig_y = [sb(f"trig_y{i}", [P, UNROLL, AR]) for i in range(2)]
        trig_x = [sb(f"trig_x{i}", [P, UNROLL, AA]) for i in range(2)]
        Y = [sb(f"y_tab{i}", [P, UNROLL, AR]) for i in range(2)]
        X = [sb(f"x_tab{i}", [P, UNROLL, AA]) for i in range(2)]
        XG = [sb(f"xg_tab{i}", [P, UNROLL, AA]) for i in range(2)]
        xprod = [sb(f"xprod{i}", [P, UNROLL, AA]) for i in range(4)]
        lam_f = sb("lam_f", [P, UNROLL, 2])
        lam_s = sb("lam_s", [P, UNROLL, 2, 2], F32R)
        waited = sb("waited", [P, 1])
        credit = sb("credit", [P, 2])
        warm = sb("warm", [P, 1])
        ps_split = [ctx.enter_context(nc.psum_tensor(f"ps_split{i}", [P, 512], F32)) for i in range(2)]
        ps_state = [ctx.enter_context(nc.psum_tensor(f"ps_state{i}", [P, 512], F32)) for i in range(2)]
        ps_y = [ctx.enter_context(nc.psum_tensor(f"ps_y{i}", [P, 512], F32)) for i in range(4)]
        k_pad = nc.dram_tensor("k_pad", [UNROLL, 2, 2, P + CH], F32, kind="Internal")

        consts_ready = sem("consts_ready")
        params_in = sem("params_in")
        len_in = sem("len_in")
        dve_step = sem("dve_step")
        act_step = sem("act_step")
        act_params = sem("act_params")
        dve_params = sem("dve_params")
        par_transposed = sem("par_transposed")
        par_ready = sem("par_ready")
        mask_consts = sem("mask_consts")
        pool_step = sem("pool_step")
        fold_ready = sem("fold_ready")
        powers_ready = sem("powers_ready")
        gain_step = sem("gain_step")
        warmed = sem("warmed")
        args_ready = sem("args_ready")
        angles_reduced = sem("angles_reduced")
        trig_ready = sem("trig_ready")
        mag_ready = sem("mag_ready")
        tables_ready = sem("tables_ready")
        lam_ready = sem("lam_ready")
        gen_ready = sem("gen_ready")
        dve_gen_step = sem("dve_gen_step")
        q_hi = sem("q_hi")
        q_split = sem("q_split")
        transposed = sem("transposed")
        hi_done = sem("hi_done")
        first_turned = sem("first_turned")
        splits = sem("splits")
        copied = sem("copied")
        turned = sem("turned")
        s_hi = sem("s_hi")
        s_split = sem("s_split")
        y_ready = sem("y_ready")
        y_out = sem("y_out")
        k_written = sem("k_written")
        written = sem("written")
        x_loaded = [sem(f"x_loaded{r}") for r in range(UNROLL)]
        t_loaded = [sem(f"t_loaded{r}") for r in range(UNROLL)]

        def first(k):
            return isinstance(k, int) and k == -1

        def final(k):
            return isinstance(k, int) and k == H - 1

        def exists(k, lead):
            return not isinstance(k, int) or k + lead < H

        INPUT_GROUPS = ((0, 1), (2,), (3,), ())
        PROLOGUE_GROUPS = ((False, 0), (False, 1), (False, 2), (False, 3), (True, 0), (True, 1))
        assert len(PROLOGUE_GROUPS) == PRO_GROUPS

        def y_no(k, d, old):
            if first(k):
                return d
            return k * 8 + (4 + d if final(k) else 4 + 2 * d + (0 if old else 1))

        def copy_no(k, d, old):
            if first(k):
                return d
            if final(k):
                return k * 7 + 4 + d
            return k * 7 + 4 + min(2 * d + (0 if old else 1), 6)

        def turn_no(k, d, old):
            if first(k):
                return d - 1
            if final(k):
                return k * 7 + (4 + d if old else 3)
            return k * 7 + (4 + 2 * d if old else 3 + 2 * d)

        def group_no(k, g):
            return k * 5 + (PRO_GROUPS + 5 + g)

        def table_pieces(k, u, d, q):
            if first(k):
                return TABLE_SLOTS[d]
            return (4 * u + d - 10,) if q is not None and 10 <= 4 * u + d < 10 + PIECES else ()

        def each_step(eng, body):
            body(-1, UNROLL - 1, None)
            with eng.Fori(0, QUADS - 1) as q:
                for u in range(UNROLL):
                    body(q * UNROLL + u, u, q)
            for u in range(UNROLL):
                body(H - UNROLL + u, u, None)

        def channel_tables(eng, quad, done):
            def times(out_, a, b):
                return eng.tensor_tensor(out_, a, b, ALU.mult)
            cols = bass.ds(quad * UNROLL, UNROLL)
            eng.wait_ge(trig_ready, done * 7 + 7)
            eng.wait_ge(mag_ready, done + 1)
            for i in range(2):
                times(Y[i][:, :, :], trig_y[i][:, :, :], mag[:, :, 0:AR]).then_inc(powers_ready, 1)
                times(X[i][:, :, :], trig_x[i][:, :, :], mag[:, :, AR:NK]).then_inc(powers_ready, 1)
            eng.wait_ge(powers_ready, done * 4 + 4)
            yield
            g1 = par[:, 2, cols].unsqueeze(2).broadcast_to([P, UNROLL, AA])
            g2 = par[:, 3, cols].unsqueeze(2).broadcast_to([P, UNROLL, AA])
            times(xprod[0][:, :, :], X[0][:, :, :], g1).then_inc(gain_step, 1)
            times(xprod[1][:, :, :], X[1][:, :, :], g2).then_inc(gain_step, 1)
            times(xprod[2][:, :, :], X[1][:, :, :], g1).then_inc(gain_step, 1)
            times(xprod[3][:, :, :], X[0][:, :, :], g2).then_inc(gain_step, 1)
            eng.wait_ge(gain_step, done * 4 + 4)
            eng.tensor_tensor(XG[0][:, :, :], xprod[0][:, :, :], xprod[1][:, :, :], ALU.add).then_inc(tables_ready, 1)
            eng.tensor_tensor(XG[1][:, :, :], xprod[2][:, :, :], xprod[3][:, :, :], ALU.subtract).then_inc(tables_ready, 1)

        def outer(eng, products, step_done, steps, dst, hi, r, n):
            hi_b = [hi[i][:, r, 0:n].unsqueeze(2).broadcast_to([P, n, AR]) for i in range(2)]
            lo_b = [Y[i][:, r, :].unsqueeze(1).broadcast_to([P, n, AR]) for i in range(2)]
            for i in range(2):
                eng.tensor_tensor(products[i][:, 0:n * AR].rearrange("p (a r) -> p a r", r=AR),
                                  hi_b[i], lo_b[i], ALU.mult).then_inc(step_done, 1)
            eng.wait_ge(step_done, steps + 2)
            eng.tensor_tensor(dst, products[0][:, 0:n * AR], products[1][:, 0:n * AR], ALU.add).then_inc(step_done, 1)

        def input_powers(eng, products, step_done, steps, r):
            forward = Wf[:, r % 2, :]
            backward = bass.AP(forward.tensor, forward.offset + (CH - 1), [list(forward.ap[0]), [-1, CH]])
            outer(eng, products, step_done, steps, backward, X, r, AA - 1)

        def readout(eng, products, step_done, steps, r):
            outer(eng, products, step_done, steps, Qf[:, r % 2, :], XG, r, AA)
            eng.wait_ge(step_done, steps + 3)

        def decay_matrix(eng, r):
            v = lam_s[:, r, :, :].bitcast(F32).unsqueeze(3).broadcast_to([P, 2, 2, N])
            m = fold[:, :].unsqueeze(1).broadcast_to([P, 2, N])
            for i in range(2):
                eng.tensor_tensor(QL[:, r, i, NQ:NQ + P].rearrange("p (a m) -> p a m", a=2), m, v[:, i, :, :],
                                  ALU.mult).then_inc(gen_ready, 1)

        block = ctx.enter_context(nc.Block())

        @block.sync
        def _(eng):
            eng.dma_start(e_in[:, 0:1], log_dt.rearrange("(h o) -> h o", o=1)).then_inc(params_in, 16)
            eng.dma_start(e_in[:, 1:1 + N], log_A_real[:, :]).then_inc(params_in, 16)
            eng.dma_start(aim[:, :], A_imag[:, :]).then_inc(params_in, 16)
            eng.dma_start(c_in[:, :, :], C[:, :, :]).then_inc(params_in, 16)
            eng.dma_start(d_in[:, :], D.rearrange("(o h) -> o h", o=1)).then_inc(params_in, 16)
            eng.dma_start(len_i[:, :], lengths.rearrange("(b o) -> b o", o=1)).then_inc(len_in, 16)
            for h in range(UNROLL - 1):
                eng.dma_start(x_sb[h][:, :], x[:, h, :]).then_inc(x_loaded[h], 16)
            eng.wait_ge(consts_ready, 1)
            for copy in range(2):
                eng.dma_start(k_pad[:, copy, :, 0:P], zero[0:UNROLL, :, :]).then_inc(written, 16)
            eng.wait_ge(written, PAD_WRITES)

            def store_k(r, group):
                eng.wait_ge(splits, group + (SPLIT_CREDIT + 1))
                eng.dma_start(k_pad[r, :, :, P:P + CH],
                              TPK[0:2, r, :, CH + 2 * P:].bitcast(F32)).then_inc(k_written, 16)

            def load_toeplitz(h, r):
                eng.wait_ge(k_written, h * 16 + 16)
                row = k_pad[r, :, :, :]
                for i in range(2):
                    skewed = bass.AP(row.tensor, row.offset + (i * (P + CH) + P),
                                     [[2 * (P + CH) - N, 2], [-1, N], [1, CH]])
                    eng.dma_start(T_of(r, i).bitcast(F32), skewed).then_inc(t_loaded[r], 16)

            def T_of(r, i):
                return TPK[:, r, i, 0:CH]

            def channel_of(tensor, h):
                return tensor[:, bass.ds(h, 1), :].rearrange("b o l -> b (o l)")

            for h in range(2):
                store_k(h, PROLOGUE_GROUPS.index((True, h)))
                load_toeplitz(h, h)

            def step(k, u, q):
                r = (u + 3) % UNROLL
                if exists(k, 3) and not first(k):
                    eng.wait_ge(written, k * 16 + PAD_WRITES)
                    eng.dma_start(x_sb[r][:, :], channel_of(x, k + 3)).then_inc(x_loaded[r], 16)
                if exists(k, 3):
                    store_k(r, group_no(k, 4))
                if not first(k):
                    for d in range(4) if final(k) else (3,):
                        eng.wait_ge(y_out, y_no(k, d, True) + (Y_CREDIT + 1))
                        cols = slice(CH * (4 + d) if final(k) and d > 0 else 0, CH * (5 + d))
                        eng.dma_start(channel_of(out, k)[:, cols], x_sb[u][:, cols]).then_inc(written, 16)
                if exists(k, 3):
                    if not first(k):
                        eng.wait_ge(y_ready, k * 8 + 4)
                    load_toeplitz(k + 3, r)

            each_step(eng, step)
            eng.wait_ge(written, (H + LAST_STORES) * 16 + PAD_WRITES)

        @block.gpsimd
        def _(eng):
            eng.memset(zero[:, :, :], 0.0).then_inc(consts_ready, 1)
            eng.memset(ident[:, :], 1.0).then_inc(pool_step, 1)
            eng.memset(ones_f[:, :], 1.0).then_inc(pool_step, 1)
            eng.memset(minus_re[:, :], 1.0).then_inc(pool_step, 1)
            eng.wait_ge(pool_step, 3)
            eng.affine_select(ident[:, :], ident[:, :], [[-1, P]], ALU.is_equal, 0.0, base=0,
                              channel_multiplier=1).then_inc(consts_ready, 1)
            eng.affine_select(minus_re[:, :], minus_re[:, :], [[0, 1]], ALU.is_ge, -1.0, base=-N,
                              channel_multiplier=1).then_inc(consts_ready, 1)
            eng.iota(kv[:, 0:AR], [[1, AR]], base=0, channel_multiplier=0,
                     allow_small_or_imprecise_dtypes=True).then_inc(consts_ready, 1)
            eng.iota(kv[:, AR:NK], [[AR, AA]], base=0, channel_multiplier=0,
                     allow_small_or_imprecise_dtypes=True).then_inc(consts_ready, 1)
            eng.memset(half_pi[:, :], HALF_PI).then_inc(consts_ready, 1)
            eng.wait_ge(consts_ready, 2)
            eng.tensor_tensor(fold[:, :], ident[:, 0:N], ident[:, N:P], ALU.add).then_inc(fold_ready, 1)
            eng.wait_ge(fold_ready, 1)
            eng.iota(pos[:, :], [[1, L]], base=0, channel_multiplier=0,
                     allow_small_or_imprecise_dtypes=True).then_inc(mask_consts, 1)

            def times(out_, a, b):
                return eng.tensor_tensor(out_, a, b, ALU.mult)

            def arguments(quad):
                cols = bass.ds(quad * UNROLL, UNROLL)
                k = kv[:, :].unsqueeze(1).broadcast_to([P, UNROLL, NK])
                times(ang[:, :, :], par[:, 1, cols].unsqueeze(2).broadcast_to([P, UNROLL, NK]), k).then_inc(args_ready, 1)
                times(dec[:, :, :], par[:, 0, cols].unsqueeze(2).broadcast_to([P, UNROLL, NK]), k).then_inc(args_ready, 1)

            def tables(quad):
                eng.wait_ge(lam_ready, quad * 2)
                for _ in channel_tables(eng, quad, quad):
                    pass

            gen_step = sem("gen_step")

            def matrices(h, r, quad, uses_before):
                input_powers(eng, prod, gen_step, h * 6 - 6, r)
                eng.wait_ge(gen_step, h * 6 - 3)
                eng.wait_ge(tables_ready, quad * 2 + 2)
                readout(eng, prod, gen_step, h * 6 - 3, r)
                if isinstance(h, int) and h == 1:
                    eng.wait_ge(gen_ready, 3)
                eng.tensor_tensor(Qf[:, r % 2, 0:1], Qf[:, r % 2, 0:1], dcol[:, bass.ds(h, 1)], ALU.add).then_inc(gen_ready, 1)
                eng.wait_ge(lam_ready, quad * 2 + 2)
                if uses_before is not None:
                    eng.wait_ge(y_ready, uses_before)
                decay_matrix(eng, r)

            eng.wait_ge(par_ready, PAR_DTA)
            arguments(0)
            for t, (is_matrices, g) in enumerate(PROLOGUE_GROUPS):
                if not is_matrices:
                    hi, lo = (U[0][i][:, 4 * g:4 * g + 4, :].rearrange("p j b -> p (j b)") for i in range(2))
                    eng.wait_ge(hi_done, t + 1)
                    eng.wait_ge(first_turned, t + 1)
                    eng.tensor_tensor(lo, UF[:, t % 2, :], hi.bitcast(F32), ALU.subtract).then_inc(splits, 1)
            eng.wait_ge(powers_ready, 4)
            matrices(1, 1, 0, None)

            def step(k, u, q):
                if first(k):
                    arguments(1)
                if exists(k, 3):
                    if not first(k):
                        eng.wait_ge(splits, group_no(k - 2, 4) + (SPLIT_CREDIT + 1))
                    else:
                        eng.wait_ge(splits, PROLOGUE_GROUPS.index((True, 0)) + (SPLIT_CREDIT + 1))
                    quad = 0 if first(k) else QUADS - 1 if q is None else q if u == 0 else q + 1
                    matrices(k + 3, (u + 3) % UNROLL, quad, None if first(k) else k * 8 + 4)
                if u == 2 and q is not None:
                    arguments(q + 2)
                if u == 0 and q is not None:
                    tables(q + 1)

            each_step(eng, step)

        @block.scalar
        def _(eng):
            def angle_tables(done, piece):
                def cos(dst, rows, ks):
                    eng.activation(dst[rows, :, :], ared[rows, :, ks], ACT.Sin, bias=half_pi[rows, :], scale=-1.0).then_inc(trig_ready, 1)
                def sin(dst, rows, ks, scale):
                    eng.activation(dst[rows, :, :], red[3][rows, :, ks], ACT.Sin, scale=scale).then_inc(trig_ready, 1)
                re, im, low, high = slice(0, N), slice(N, P), slice(0, AR), slice(AR, NK)
                if piece == 0:
                    eng.wait_ge(args_ready, done * 2 + 2)
                    eng.activation(th[:, :, :], dec[:, :, :], ACT.Tanh, scale=0.5).then_inc(trig_ready, 1)
                elif piece == 3:
                    eng.wait_ge(angles_reduced, done + 1)
                    eng.activation(ared[:, :, :], red[3][:, :, :], ACT.Abs).then_inc(act_step, 1)
                    sin(trig_y[0], im, low, 1.0)
                    sin(trig_y[1], re, low, 1.0)
                    sin(trig_x[1], slice(0, P), high, minus_re[:, 0:1])
                elif piece == 4:
                    eng.wait_ge(act_step, done + 1)
                    cos(trig_y[0], re, low)
                    cos(trig_y[1], im, low)
                    cos(trig_x[0], slice(0, P), high)

            eng.wait_ge(consts_ready, 6)
            eng.activation(warm[:, :], half_pi[:, :], ACT.Silu).then_inc(warmed, 1)
            eng.activation(ones[:, :], ones_f[:, :], ACT.Copy).then_inc(act_params, 1)
            eng.wait_ge(dve_params, 2)
            eng.activation(pt[0][:, :], par_h[:, 0, 0, :], ACT.Tanh, scale=0.5).then_inc(act_params, 1)
            eng.wait_ge(par_transposed, 2)
            eng.activation(par[:, 0:2, 0:H], ps_y[0][:, 0:2 * H].rearrange("p (i h) -> p i h", i=2), ACT.Copy).then_inc(par_ready, 1)
            eng.wait_ge(dve_params, 3)
            eng.activation(pt[4][:, :], pt[3][:, :], ACT.Abs).then_inc(act_params, 1)
            eng.activation(pt[5][:, :], pt[3][:, :], ACT.Sin).then_inc(act_params, 1)
            eng.activation(pt[6][:, :], pt[3][:, :], ACT.Sin, scale=0.5).then_inc(act_params, 1)
            eng.wait_ge(act_params, 3)
            eng.activation(pt[7][:, :], pt[4][:, :], ACT.Sin, bias=half_pi[0:H, :], scale=-1.0).then_inc(act_params, 1)
            angle_tables(0, 0)

            def split_hi(t, b, dst):
                eng.wait_ge(transposed, t + 1)
                eng.activation(dst, ps_split[b][:, :], ACT.Copy).then_inc(hi_done, 1)

            def q_hi_of(h, r):
                eng.wait_ge(gen_ready, h * 3 + 1)
                eng.activation(QK[0:N, r % 2, :], Qf[0:N, r % 2, 0:CH], ACT.Copy)
                eng.activation(QL[:, r, 0, 0:NQ], Qf[:, r % 2, 0:NQ], ACT.Copy).then_inc(q_hi, 1)

            def u_hi(g, r):
                return U[r][0][:, 4 * g:4 * g + 4, :].rearrange("p j b -> p (j b)")

            for t, (is_matrices, i) in enumerate(PROLOGUE_GROUPS):
                if is_matrices:
                    if i == 0:
                        for piece in (3, 4):
                            angle_tables(0, piece)
                    q_hi_of(i, i)
                split_hi(t, t % 2, TPK[:, i, 0, CH:] if is_matrices else u_hi(i, 0))
                if not is_matrices:
                    eng.activation(UF[:, t % 2, :], ps_split[t % 2][:, :], ACT.Copy).then_inc(first_turned, 1)

            def step(k, u, q):
                pk = k if q is None else u

                def state_copy(d, old):
                    eng.wait_ge(y_ready, y_no(k, d, old) + 1)
                    eng.activation(ST[:, copy_no(pk, d, old) % 2, :], ps_y[y_no(pk, d, old) % 4][:, CH:CH + P],
                                   ACT.Copy).then_inc(copied, 1)

                def state_hi(d, old):
                    n, pn = turn_no(k, d, old), turn_no(pk, d, old)
                    eng.wait_ge(turned, n + 1)
                    eng.activation(S[:, pn % 4, 0, :], ps_state[pn % 2][:, 0:P], ACT.Copy).then_inc(s_hi, 1)

                if not first(k):
                    eng.wait_ge(y_ready, k * 8 + 4)
                for d in range(4):
                    if not (first(k) and d == 0) and not (final(k) and d > 0):
                        state_hi(d, False)
                    if d > 0 and not first(k) and d < 3:
                        state_copy(d, True)
                    if exists(k, 2):
                        for g in INPUT_GROUPS[d]:
                            split_hi(group_no(k, g), group_no(pk, g) % 2, u_hi(g, (u + 2) % UNROLL))
                    if d == 0 and not first(k):
                        state_copy(d, True)
                    if d == 3 and exists(k, 3):
                        split_hi(group_no(k, 4), group_no(pk, 4) % 2, TPK[:, (u + 3) % UNROLL, 0, CH:])
                    if not first(k) and d < 3:
                        state_hi(d, True)
                    if not final(k):
                        state_copy(d, False)
                    if d == 1 and exists(k, 3):
                        q_hi_of(k + 3, (u + 3) % UNROLL)
                    for piece in table_pieces(k, u, d, q):
                        angle_tables(1 if first(k) else q + 2, piece)

            each_step(eng, step)

        @block.vector
        def _(eng):
            count = [0]

            def step(*operations):
                for ins in operations:
                    count[0] += 1
                    ins.then_inc(dve_step, 1)
                eng.wait_ge(dve_step, count[0])

            tt, ts, stt = eng.tensor_tensor, eng.tensor_scalar, eng.scalar_tensor_tensor

            def reduce_angle(i, ang_, t0, t1, r):
                if i == 0:
                    return eng.tensor_scalar(t0, ang_, INV_2PI, MAGIC, ALU.mult, ALU.add)
                if i == 1:
                    return eng.tensor_scalar(t1, t0, MAGIC, None, ALU.subtract)
                if i < 5:
                    return eng.scalar_tensor_tensor(r[i - 2], t1, -TWO_PI[i - 2], ang_ if i == 2 else r[i - 3], ALU.mult, ALU.add)
                return eng.tensor_scalar(r[3], r[2], PI_BELOW, -PI_BELOW, ALU.min, ALU.max)

            eng.memset(dcol[:, :], 0.0).then_inc(dve_step, 1)
            count[0] = 1
            eng.memset(credit[:, 0:1], 0.0).then_inc(splits, SPLIT_CREDIT)
            eng.memset(par[:, :, H:HP], 0.0).then_inc(par_ready, 1)
            eng.wait_ge(params_in, 80)
            e, f, n_ = (t[:, :] for t in e_t)
            step(ts(e_in[:, :], e_in[:, :], 88.0, -87.0, ALU.min, ALU.max))
            step(ts(f, e_in[:, :], LOG2E, MAGIC, ALU.mult, ALU.add))
            step(ts(n_, f, MAGIC, None, ALU.subtract))
            step(stt(e, n_, -LN2[0], e_in[:, :], ALU.mult, ALU.add))
            step(stt(e_in[:, :], n_, -LN2[1], e, ALU.mult, ALU.add))
            step(ts(f, e_in[:, :], EXP_POLY[0], None, ALU.mult),
                 ts(n_, n_, 127.0, 8388608.0, ALU.add, ALU.mult))
            step(stt(f, f, EXP_POLY[1], e_in[:, :], ALU.add, ALU.mult),
                 eng.tensor_copy(e_i[:, :], n_))
            for a in EXP_POLY[2:]:
                step(stt(f, f, a, e_in[:, :], ALU.add, ALU.mult))
            step(stt(e_out[:, :], f, 1.0, e_i[:, :].bitcast(F32), ALU.add, ALU.mult))
            dt, aexp = e_out[:, 0:1], e_out[:, 1:1 + N]
            p = [t[:, :] for t in pt]
            a_re, a_im = p[8], aim[:, :]
            step(ts(a_re, aexp, -1.0, None, ALU.mult))
            for i, a in enumerate((a_re, a_im)):
                ts(par_h[:, i, :, :], a.unsqueeze(1).broadcast_to([H, 2, N]), dt, None, ALU.mult).then_inc(dve_params, 1)
            eng.wait_ge(dve_params, 2)
            reduced = (par_h[:, 1, 0, :], p[1], p[2], [p[9], p[10], p[11], p[3]])
            square, norm, inv_norm = pair[0][:, 0, :], pair[0][:, 1, :], pair[1][:, 0, :]
            step(reduce_angle(0, *reduced), tt(square, a_re, a_re, ALU.mult), tt(norm, a_im, a_im, ALU.mult))
            step(reduce_angle(1, *reduced), tt(square, square, norm, ALU.add))
            step(reduce_angle(2, *reduced), eng.reciprocal(inv_norm, square))
            step(reduce_angle(3, *reduced))
            step(reduce_angle(4, *reduced))
            reduce_angle(5, *reduced).then_inc(dve_params, 1)

            def both(v):
                return v.unsqueeze(1).broadcast_to([H, 2, N])

            table = (ang[:, :, :], turns[:, :, :], turns_r[:, :, :], [r[:, :, :] for r in red])
            z, t1, t2, quot, gain = (t[:, :, :] for t in (pair[2], pair[3], pair[4], pair[5], pair[6]))
            eng.wait_ge(act_params, 2)
            step(ts(p[1], p[0], -1.0, 1.0, ALU.mult, ALU.add))
            eng.wait_ge(args_ready, 2)
            step(eng.reciprocal(p[2], p[1]), reduce_angle(0, *table))
            step(stt(p[1], p[0], 2.0, p[2], ALU.mult, ALU.mult), reduce_angle(1, *table))
            eng.wait_ge(act_params, 6)
            step(stt(z[:, 1, :], p[1], 1.0, p[5], ALU.add, ALU.mult),
                 tt(p[9], p[1], p[7], ALU.mult),
                 stt(p[10], p[6], -2.0, p[6], ALU.mult, ALU.mult), reduce_angle(2, *table))
            step(tt(z[:, 0, :], p[9], p[10], ALU.add), reduce_angle(3, *table))
            step(tt(t1, z, both(a_re), ALU.mult), tt(t2, z, both(a_im), ALU.mult), reduce_angle(4, *table))
            step(tt(quot[:, 0, :], t1[:, 0, :], t2[:, 1, :], ALU.add), tt(quot[:, 1, :], t1[:, 1, :], t2[:, 0, :], ALU.subtract))
            reduce_angle(5, *table).then_inc(angles_reduced, 1)
            step(tt(quot, quot, both(inv_norm), ALU.mult))
            cre, cim = (c_in[:, :, i:i + 1].rearrange("h n o -> h (n o)") for i in range(2))
            step(tt(t1, quot, both(cre), ALU.mult), tt(t2, quot, both(cim), ALU.mult))
            step(tt(gain[:, 0, :], t1[:, 0, :], t2[:, 1, :], ALU.subtract), tt(gain[:, 1, :], t1[:, 1, :], t2[:, 0, :], ALU.add))
            ts(par_h[:, 2, 0, :], gain[:, 0, :], 2.0, None, ALU.mult).then_inc(dve_params, 1)
            ts(par_h[:, 2, 1, :], gain[:, 0, :], -2.0, None, ALU.mult).then_inc(dve_params, 1)
            for half in range(2):
                ts(par_h[:, 3, half, :], gain[:, 1, :], 2.0, None, ALU.mult).then_inc(dve_params, 1)
            ts(dcol[0:1, 0:H], d_in[:, :], 1.0, None, ALU.add).then_inc(par_ready, 1)

            tab_step = sem("tab_step")

            def reduce_and_magnitudes(done, piece):
                if piece < 3:
                    if piece == 0:
                        eng.wait_ge(args_ready, done * 2 + 2)
                    for i in (2 * piece, 2 * piece + 1):
                        if i > 0:
                            eng.wait_ge(tab_step, done * 8 + i)
                        ins = reduce_angle(i, ang[:, :, :], turns[:, :, :], turns_r[:, :, :], [r[:, :, :] for r in red])
                        ins.then_inc(angles_reduced if i == 5 else tab_step, 1)
                    return
                if piece == 3:
                    eng.wait_ge(trig_ready, done * 7 + 1)
                    eng.tensor_scalar(th_u[:, :, :], th[:, :, :], -1.0, 1.0, ALU.mult, ALU.add).then_inc(tab_step, 1)
                    eng.wait_ge(tab_step, done * 8 + 6)
                    eng.reciprocal(th_r[:, :, 0:AR], th_u[:, :, 0:AR]).then_inc(tab_step, 1)
                else:
                    eng.reciprocal(th_r[:, :, AR:NK], th_u[:, :, AR:NK]).then_inc(tab_step, 1)
                    eng.wait_ge(tab_step, done * 8 + 8)
                    eng.scalar_tensor_tensor(mag[:, :, :], th[:, :, :], 1.0, th_r[:, :, :], ALU.add, ALU.mult).then_inc(mag_ready, 1)

            lam_step = sem("lam_step")

            def decay_scalars(done):
                eng.wait_ge(powers_ready, done * 4 + 4)
                if not (isinstance(done, int) and done == 0):
                    eng.wait_ge(gen_ready, done * 12)
                re, im, k256 = slice(0, N), slice(N, P), slice(AA - 1, AA)
                eng.tensor_copy(lam_f[re, :, 0:1], X[0][re, :, k256]).then_inc(lam_step, 1)
                eng.tensor_scalar(lam_f[im, :, 0:1], X[1][im, :, k256], -1.0, None, ALU.mult).then_inc(lam_step, 1)
                eng.tensor_scalar(lam_f[re, :, 1:2], X[1][re, :, k256], -1.0, None, ALU.mult).then_inc(lam_step, 1)
                eng.tensor_copy(lam_f[im, :, 1:2], X[0][im, :, k256]).then_inc(lam_step, 1)
                eng.wait_ge(lam_step, done * 4 + 4)
                eng.tensor_copy(lam_s[:, :, 0, :], lam_f[:, :, :]).then_inc(lam_ready, 1)
                eng.wait_ge(lam_ready, done * 2 + 1)
                eng.tensor_tensor(lam_s[:, :, 1, :], lam_f[:, :, :], lam_s[:, :, 0, :].bitcast(F32), ALU.subtract).then_inc(lam_ready, 1)

            def split_lo(t, b, dst, hi):
                eng.wait_ge(hi_done, t + 1)
                eng.tensor_tensor(dst, ps_split[b][:, :], hi.bitcast(F32), ALU.subtract).then_inc(splits, 1)

            def k_lo_of(h, r):
                eng.wait_ge(q_hi, h + 1)
                eng.tensor_tensor(QK[N:P, r % 2, :], Qf[0:N, r % 2, 0:CH], QL[0:N, r, 0, 0:CH].bitcast(F32), ALU.subtract)

            def q_lo_of(r):
                eng.tensor_tensor(QL[:, r, 1, 0:NQ], Qf[:, r % 2, 0:NQ], QL[:, r, 0, 0:NQ].bitcast(F32),
                                  ALU.subtract).then_inc(q_split, 1)

            def matrices_lo(t, b, r):
                split_lo(t, b, TPK[:, r, 1, CH:], TPK[:, r, 0, CH:])

            def u_lo(t, b, g, r):
                hi, lo = (U[r][i][:, 4 * g:4 * g + 4, :].rearrange("p j b -> p (j b)") for i in range(2))
                split_lo(t, b, lo, hi)

            eng.memset(waited[:, :], 0.0).then_inc(tab_step, 5)
            for piece in (3, 4):
                reduce_and_magnitudes(0, piece)
            first_tables = channel_tables(eng, 0, 0)
            next(first_tables)
            input_powers(eng, dve_prod, dve_gen_step, 0, 0)
            eng.wait_ge(par_transposed, 4)
            eng.tensor_copy(par[:, 2:4, 0:H], ps_y[0][:, 2 * H:4 * H].rearrange("p (i h) -> p i h", i=2)).then_inc(par_ready, 1)
            eng.wait_ge(par_ready, PAR_ALL)
            eng.memset(credit[:, 1:2], 0.0).then_inc(y_out, Y_CREDIT)
            for _ in first_tables:
                pass
            eng.wait_ge(dve_gen_step, 3)
            eng.wait_ge(tables_ready, 2)
            readout(eng, dve_prod, dve_gen_step, 3, 0)
            tt(Qf[:, 0, 0:1], Qf[:, 0, 0:1], dcol[:, 0:1], ALU.add).then_inc(gen_ready, 1)
            def first_mask():
                eng.wait_ge(len_in, 16)
                eng.wait_ge(mask_consts, 1)
                eng.tensor_copy(len_f[:, :], len_i[:, :]).then_inc(mask_consts, 1)
                eng.wait_ge(mask_consts, 2)
                ts(mask[:, :], pos[:, :], len_f[:, 0:1], None, ALU.is_lt).then_inc(mask_consts, 1)
                eng.wait_ge(mask_consts, 3)

            for t, (is_matrices, i) in enumerate(PROLOGUE_GROUPS):
                if is_matrices:
                    k_lo_of(i, i)
                    q_lo_of(i)
                    if i == 0:
                        decay_scalars(0)
                        eng.wait_ge(lam_ready, 2)
                        eng.wait_ge(fold_ready, 1)
                        decay_matrix(eng, 0)
                        eng.wait_ge(splits, t + SPLIT_CREDIT)
                    matrices_lo(t, t % 2, i)
            first_mask()

            def step(k, u, q):
                pk = k if q is None else u

                def state_lo(d, old):
                    n, pn = turn_no(k, d, old), turn_no(pk, d, old)
                    eng.wait_ge(s_hi, n + 1)
                    eng.tensor_tensor(S[:, pn % 4, 1, :], ps_state[pn % 2][:, 0:P], S[:, pn % 4, 0, :].bitcast(F32),
                                      ALU.subtract).then_inc(s_split, 1)

                def output(channel_place, c, number):
                    cols = slice(CH * c, CH * (c + 1))
                    eng.copy_predicated(x_sb[channel_place][:, cols], mask[:, cols], ps_y[number % 4][:, 0:CH]).then_inc(y_out, 1)

                for d in range(4):
                    if not (first(k) and d == 0) and not (final(k) and d > 0):
                        state_lo(d, False)
                        if d == 0:
                            output(u, 3, 3)
                        else:
                            output((u + 1) % UNROLL, d - 1, y_no(pk, d - 1, False))
                    if d == 2 and exists(k, 3):
                        q_lo_of((u + 3) % UNROLL)
                    if exists(k, 2):
                        for g in INPUT_GROUPS[d]:
                            u_lo(group_no(k, g), group_no(pk, g) % 2, g, (u + 2) % UNROLL)
                    if not first(k) and d < 3:
                        state_lo(d, True)
                        output(u, 4 + d, y_no(pk, d, True))
                    if d == 1 and exists(k, 3):
                        k_lo_of(k + 3, (u + 3) % UNROLL)
                    if d == 3 and u == 0 and q is not None:
                        decay_scalars(q + 1)
                    if d == 3 and exists(k, 3):
                        matrices_lo(group_no(k, 4), group_no(pk, 4) % 2, (u + 3) % UNROLL)
                    for piece in table_pieces(k, u, d, q):
                        reduce_and_magnitudes(1 if first(k) else q + 2, piece)
                if not first(k):
                    eng.wait_ge(y_ready, y_no(k, 3, True) + 1)
                    eng.memset(waited[:, :], 0.0)
                    output(u, 7, y_no(pk, 3, True))

            each_step(eng, step)

        @block.tensor
        def _(eng):
            def product(dst, lhs, rhs, first, passes=range(3)):
                for i in passes:
                    ins = eng.matmul(dst, lhs[i == 2], rhs[i == 1], start=first and i == 0, stop=i == 2, skip_group_check=True)
                return ins

            eng.wait_ge(consts_ready, 6)
            def parameters(i):
                eng.transpose(ps_y[0][:, i * H:(i + 1) * H], par_h[:, i, :, :].rearrange("h a n -> h (a n)"),
                              ident[0:H, 0:H]).then_inc(par_transposed, 1)

            eng.wait_ge(dve_params, 2)
            for i in range(2):
                parameters(i)

            def matrices_group(h, r, t, b):
                eng.wait_ge(q_split, h + 1)
                eng.wait_ge(splits, t + 1)
                for j in range(2):
                    eng.transpose(ps_split[b][:, P * j:P * (j + 1)], Wf[:, r % 2, P * j:P * (j + 1)], ident[:, :])
                eng.matmul(ps_split[b][:, CH:2 * CH], ones[:, :], QK[:, r % 2, :], start=True, stop=True,
                           skip_group_check=True).then_inc(transposed, 1)

            def input_group(g, r, t, b):
                eng.wait_ge(splits, t + 1)
                for j in range(4):
                    J = 4 * g + j
                    ins = eng.transpose(ps_split[b][:, P * j:P * (j + 1)], x_sb[r][:, P * J:P * (J + 1)], ident[:, :])
                ins.then_inc(transposed, 1)

            def first_block(bank, r, c):
                n = CH + P if c < NCH - 1 else CH
                product(bank[:, 0:n], [U[r][i][:, 2 * c, :] for i in range(2)],
                        [TPK[:, r, i, 0:n] for i in range(2)], True)

            def second_block(bank, r, c, passes=range(3)):
                if c < NCH - 1:
                    rhs = [TPK[:, r, i, 0:CH + 2 * P].rearrange("p (a n) -> p a n", n=P)[:, 0:4:3, :] for i in range(2)]
                    dst = bank[:, P:P + CH].rearrange("p (a n) -> p a n", n=P)
                else:
                    rhs, dst = [TPK[:, r, i, 0:P] for i in range(2)], bank[:, P:CH]
                return product(dst, [U[r][i][:, 2 * c + 1, :] for i in range(2)], rhs, False, passes)

            def state_product(bank, place, r, c):
                n = CH + P if c < NCH - 1 else CH
                return product(bank[:, 0:n], [S[:, place, i, :] for i in range(2)],
                               [QL[:, r, i, 1:1 + n] for i in range(2)], False)

            eng.wait_ge(act_params, 1)
            eng.wait_ge(x_loaded[0], 16)
            for t, (is_matrices, i) in enumerate(PROLOGUE_GROUPS):
                if is_matrices:
                    if i == 0:
                        eng.wait_ge(dve_params, 7)
                        for j in range(2, 4):
                            parameters(j)
                    matrices_group(i, i, t, t % 2)
                else:
                    input_group(i, 0, t, t % 2)

            def step(k, u, q):
                pk = k if q is None else u
                quad = QUADS - 1 if q is None else q

                def turn(d, old):
                    n, pn = turn_no(k, d, old), turn_no(pk, d, old)
                    eng.wait_ge(copied, n + 1)
                    if not (isinstance(n, int) and n < 2):
                        eng.wait_ge(s_split, n - 1)
                    eng.transpose(ps_state[pn % 2][:, 0:P], ST[:, pn % 2, :], ident[:, :]).then_inc(turned, 1)

                def begin(d, old):
                    n, pn = y_no(k, d, old), y_no(pk, d, old)
                    c, r = (4 + d, u) if old else (d, (u + 1) % UNROLL)
                    eng.wait_ge(y_out, n + 1)
                    first_block(ps_y[pn % 4], r, c)
                    if d == 0 and old:
                        second_block(ps_y[pn % 4], r, c, (0, 1))
                        turn(d, False)
                        return second_block(ps_y[pn % 4], r, c, (2,))
                    return second_block(ps_y[pn % 4], r, c)

                def complete(d, old):
                    pn = y_no(pk, d, old)
                    c, r = (4 + d, u) if old else (d, (u + 1) % UNROLL)
                    m, pm = (turn_no(j, d - 1 if old and d > 0 else d, old and d > 0) for j in (k, pk))
                    eng.wait_ge(s_split, m + 1)
                    state_product(ps_y[pn % 4], pm % 4, r, c).then_inc(y_ready, 1)

                def input_groups(d):
                    if exists(k, 2):
                        if d == 0:
                            eng.wait_ge(x_loaded[(u + 2) % UNROLL], 16 if first(k) else (quad + (u >= 2)) * 16 + 16)
                        for g in INPUT_GROUPS[d]:
                            input_group(g, (u + 2) % UNROLL, group_no(k, g), group_no(pk, g) % 2)

                for d in range(4):
                    if not first(k):
                        begin(d, True)
                    if d == 0:
                        input_groups(d)
                        if not first(k):
                            complete(d, True)
                    else:
                        if first(k):
                            input_groups(d)
                        if not final(k):
                            turn(d, False)
                        if not first(k):
                            complete(d, True)
                            input_groups(d)
                    if d == 3 and exists(k, 3):
                        matrices_group(k + 3, (u + 3) % UNROLL, group_no(k, 4), group_no(pk, 4) % 2)
                    if not final(k):
                        if d == 0:
                            eng.wait_ge(splits, (PRO_GROUPS if first(k) else group_no(k - 1, 3) + 1) + SPLIT_CREDIT)
                            eng.wait_ge(t_loaded[(u + 1) % UNROLL], 32 if first(k) else (quad + (u == 3)) * 32 + 32)
                            eng.wait_ge(gen_ready, k * 3 + 6)
                        ins = begin(d, False)
                        if d == 0:
                            ins.then_inc(y_ready, 1)
                    if not first(k) and d < 3:
                        turn(d, True)
                    if not final(k) and d > 0:
                        complete(d, False)

            each_step(eng, step)


_INS = ["x", "itok_B_8_3872", "L0_cond_log_dt", "L0_cond_C", "L0_cond_log_A_real", "L0_cond_A_imag", "L0_cond_D"]


def kernel(**inputs):
    import numpy as np
    import concourse.bacc as bacc
    from concourse.bass_utils import run_bass_kernel_spmd

    nc = bacc.Bacc("TRN2", target_bir_lowering=False, num_devices=1)
    arrays, args = {}, []
    for name in _INS:
        a = np.ascontiguousarray(inputs[name])
        arrays[f"in_{name}"] = a
        args.append(nc.dram_tensor(f"in_{name}", a.shape, mybir.dt.from_np(a.dtype), kind="ExternalInput").ap())
    shape = arrays["in_x"].shape
    out = nc.dram_tensor("out_0", shape, F32, kind="ExternalOutput").ap()
    build(nc, *args, out)
    r = run_bass_kernel_spmd(nc, [arrays], core_ids=[0])
    return r.results[0]["out_0"]
```
